# Optimizing a Trainium2 kernel written in Bass

```python
import numpy as np
import jax
import jax.numpy as jnp

def _softmax(x, axis=-1):
    return jax.nn.softmax(x, axis=axis)

def _gelu(x):
    return jax.nn.gelu(x, approximate=True)

def _silu(x):
    return jax.nn.silu(x)

def _sigmoid(x):
    return jax.nn.sigmoid(x)

def _layernorm(x, axis=-1, eps=1e-05):
    m = jnp.mean(x, axis=axis, keepdims=True)
    v = jnp.var(x, axis=axis, keepdims=True)
    return (x - m) / jnp.sqrt(v + eps)

def _scatter_add(tgt, idx, src, axis=0):
    return tgt.at[idx].add(src)

def _segment_sum(src, seg, n):
    return jax.ops.segment_sum(src, seg, n)
kernel_name = 'mk_cond_seq_d1_seqx_r4_3995c1'

def setup_inputs(seed: int=0):
    np.random.seed(seed)
    _w = jnp.asarray

    def _rec_inputs():
        import jax
        import jax.numpy as jnp
        _rk = jax.random.key(seed)
        x = 7.22e-05 + 1 * jax.random.normal(jax.random.fold_in(_rk, 1), (8, 512, 256), jnp.float32)
        _lenS = 512 - jax.random.randint(jax.random.fold_in(_rk, 7), (8,), 0, max(1, 512 // 4) + 1, jnp.int32)
        _lenS2 = 512 - jax.random.randint(jax.random.fold_in(_rk, 8), (8,), 0, max(1, 512 // 4) + 1, jnp.int32)
        cond_2048 = 0.00386106 + 1.00199 * jax.random.normal(jax.random.fold_in(_rk, 11), (8, 512), jnp.float32)
        _validS = jnp.arange(512)[None, :] < _lenS[:, None]
        _validS2 = jnp.arange(512)[None, :] < _lenS2[:, None]
        _causal = jnp.tril(jnp.ones((512, 512), dtype=bool))
        mask_BxS_ff1 = jnp.where(jnp.ones((8, 512), dtype=bool), 1.0, 0.0).astype(jnp.float32)
        return (x, cond_2048, mask_BxS_ff1)
    x, cond_2048, mask_BxS_ff1 = _rec_inputs()

    def _L0_cond_setup():
        import jax, jax.numpy as jnp
        import numpy as np
        B, T, D, H, TE = (8, 256, 256, 16, 512)
        LN_EPS = 1e-05

        def layer_norm(x, w, b):
            m = jnp.mean(x, axis=-1, keepdims=True)
            v = jnp.var(x, axis=-1, keepdims=True)
            return (x - m) / jnp.sqrt(v + LN_EPS) * w + b
        key = jax.random.key(seed)
        ks = jax.random.split(key, 8)
        s = lambda k, sh: jax.random.normal(k, sh, jnp.float32) * 0.02
        return dict(x=jax.random.normal(ks[0], (B, T, D), jnp.float32), emb=jax.random.normal(ks[1], (B, TE), jnp.float32), src_mask=jnp.ones((B, T), jnp.float32), norm_w=jnp.ones((D,), jnp.float32), norm_b=jnp.zeros((D,), jnp.float32), q_w=s(ks[2], (D, D)), q_b=jnp.zeros((D,), jnp.float32), k_w=s(ks[3], (D, D)), k_b=jnp.zeros((D,), jnp.float32), v_w=s(ks[4], (D, D)), v_b=jnp.zeros((D,), jnp.float32), emb_w=s(ks[5], (TE, 2 * D)), emb_b=jnp.zeros((2 * D,), jnp.float32), sb_norm_w=jnp.ones((D,), jnp.float32), sb_norm_b=jnp.zeros((D,), jnp.float32), out_w=s(ks[6], (D, D)), out_b=jnp.zeros((D,), jnp.float32))
    _L0_cond_all = _L0_cond_setup()
    _L0_cond_in = {k: v for k, v in _L0_cond_all.items() if k in ('norm_w', 'norm_b', 'q_w', 'q_b', 'k_w', 'k_b', 'v_w', 'v_b', 'emb_w', 'emb_b', 'sb_norm_w', 'sb_norm_b', 'out_w', 'out_b')}
    del _L0_cond_all
    return {'x': x, 'cond_2048': cond_2048, 'mask_BxS_ff1': mask_BxS_ff1, 'L0_cond_norm_w': _L0_cond_in['norm_w'], 'L0_cond_norm_b': _L0_cond_in['norm_b'], 'L0_cond_q_w': _L0_cond_in['q_w'], 'L0_cond_q_b': _L0_cond_in['q_b'], 'L0_cond_k_w': _L0_cond_in['k_w'], 'L0_cond_k_b': _L0_cond_in['k_b'], 'L0_cond_v_w': _L0_cond_in['v_w'], 'L0_cond_v_b': _L0_cond_in['v_b'], 'L0_cond_emb_w': _L0_cond_in['emb_w'], 'L0_cond_emb_b': _L0_cond_in['emb_b'], 'L0_cond_sb_norm_w': _L0_cond_in['sb_norm_w'], 'L0_cond_sb_norm_b': _L0_cond_in['sb_norm_b'], 'L0_cond_out_w': _L0_cond_in['out_w'], 'L0_cond_out_b': _L0_cond_in['out_b']}

def reference(x, cond_2048, mask_BxS_ff1, L0_cond_norm_w, L0_cond_norm_b, L0_cond_q_w, L0_cond_q_b, L0_cond_k_w, L0_cond_k_b, L0_cond_v_w, L0_cond_v_b, L0_cond_emb_w, L0_cond_emb_b, L0_cond_sb_norm_w, L0_cond_sb_norm_b, L0_cond_out_w, L0_cond_out_b):
    import jax
    import jax.numpy as jnp

    def _L0_cond_ref(x, emb, src_mask, norm_w, norm_b, q_w, q_b, k_w, k_b, v_w, v_b, emb_w, emb_b, sb_norm_w, sb_norm_b, out_w, out_b):
        import jax, jax.numpy as jnp
        import numpy as np
        B, T, D, H, TE = (8, 256, 256, 16, 512)
        LN_EPS = 1e-05

        def layer_norm(x, w, b):
            m = jnp.mean(x, axis=-1, keepdims=True)
            v = jnp.var(x, axis=-1, keepdims=True)
            return (x - m) / jnp.sqrt(v + LN_EPS) * w + b
        Bx, Tx, Dx = x.shape
        xn = layer_norm(x, norm_w, norm_b)
        q = (xn @ q_w + q_b).reshape(Bx, Tx, H, -1)
        k = (xn @ k_w + k_b).reshape(Bx, Tx, H, -1)
        att = jnp.einsum('bnhl,bmhl->bnmh', q, k)
        mask = src_mask.reshape(Bx, 1, Tx, 1)
        att = att + (1.0 - mask) * -1000000.0
        att = jax.nn.softmax(att, axis=2)
        v = ((xn @ v_w + v_b) * src_mask[:, :, None]).reshape(Bx, Tx, H, -1)
        y = jnp.einsum('bnmh,bmhl->bnhl', att, v).reshape(Bx, Tx, Dx)
        e = jax.nn.silu(emb) @ emb_w + emb_b
        scale, shift = jnp.split(e[:, None, :], 2, axis=2)
        h = layer_norm(y, sb_norm_w, sb_norm_b) * (1.0 + scale) + shift
        h = jax.nn.silu(h) @ out_w + out_b
        return x + h
    x = _L0_cond_ref(x, cond_2048, mask_BxS_ff1, L0_cond_norm_w, L0_cond_norm_b, L0_cond_q_w, L0_cond_q_b, L0_cond_k_w, L0_cond_k_b, L0_cond_v_w, L0_cond_v_b, L0_cond_emb_w, L0_cond_emb_b, L0_cond_sb_norm_w, L0_cond_sb_norm_b, L0_cond_out_w, L0_cond_out_b)
    return x

_drawn_inputs = setup_inputs


def setup_inputs(seed=0):
    import zlib

    import numpy as np

    out = dict(_drawn_inputs(seed))
    spreads = {'L0_cond_norm_w': (1.0, 0.6),
     'L0_cond_norm_b': (0.0, 0.272),
     'L0_cond_q_b': (0.0, 0.8),
     'L0_cond_k_b': (0.0, 2.0),
     'L0_cond_v_b': (0.0, 0.1),
     'L0_cond_emb_b': (0.0, 0.1),
     'L0_cond_sb_norm_w': (1.0, 0.2),
     'L0_cond_sb_norm_b': (0.0, 0.364),
     'L0_cond_out_b': (0.0, 0.1)}
    factors = {'L0_cond_q_w': 2.667}
    for name, (base, spread) in spreads.items():
        noise = np.random.default_rng([zlib.crc32(name.encode()), seed]).standard_normal(out[name].shape)
        drawn = base * np.exp(spread * noise) if base else spread * noise
        out[name] = jnp.asarray(drawn.astype(out[name].dtype))
    for name, factor in factors.items():
        out[name] = (out[name] * factor).astype(out[name].dtype)
    return out
```

```python
from contextlib import ExitStack

import concourse.bass as bass
from concourse import mybir

F32 = mybir.dt.float32
BF16 = mybir.dt.bfloat16
ALU = mybir.AluOpType
ACT = mybir.ActivationFunctionType
AXIS_X = mybir.AxisListType.X

P = 128
B, T, D = 8, 512, 256
HEADS = 16
HD = D // HEADS
TE = 512
EPS = 1e-5
MASKED = 1000000.0
CH = T // P
KD = D // P
KE = TE // P
GH = 4
NG = HEADS // GH
GC = GH * HD
STEPS = NG * CH
UNITS = STEPS * GH
MAX_LEAD = 7
P_SLOTS = 4
ST_BANKS = 3
MX_BANKS = 2
PARTS = 3
ROWS_PROD = 6 * HD
ROWS_MASK = ROWS_PROD + PARTS
ROWS_ALL = ROWS_MASK + 2
VW = 32

JOBS = [
    (0, "proj", 3, 0), (1, "cturn", 1, 0), (1, "yturn", 3, -1), (3, "xturn", 0, 1), (3, "xturn", 1, 1),
    (4, "proj", 0, 1), (5, "cturn", 2, 0), (5, "yturn", 0, 0), (6, "hturn", 0, -1), (7, "hturn", 1, -1),
    (8, "proj", 1, 1), (9, "cturn", 3, 0), (9, "yturn", 1, 0), (10, "outp", 0, -1), (11, "outp", 1, -1),
    (12, "proj", 2, 1), (13, "cturn", 4, 0), (13, "yturn", 2, 0), (14, "vproj", 0, 1), (15, "vproj", 1, 1),
]


def exists(batch):
    return not isinstance(batch, int) or 0 <= batch < B


def job_exists(kind, i, db, b):
    if kind == "cturn" and i == NG:
        return exists(b + 1)
    return exists(b + db)


def wait(engine, semaphore, count):
    if not isinstance(count, int) or count > 0:
        engine.wait_ge(semaphore, count)


def wait_apart(engine, met, semaphore, count):
    if not isinstance(count, int):
        engine.wait_ge(met, 1)
    wait(engine, semaphore, count)


def attention_layer(nc, x, cond, mask, norm_w, norm_b, q_w, q_b, k_w, k_b, v_w, v_b,
                    emb_w, emb_b, sb_w, sb_b, out_w, out_b, out):
    with ExitStack() as ctx:
        def sb(name, shape, dt=F32):
            return ctx.enter_context(nc.sbuf_tensor(name, shape, dt))

        def psum(name, shape, dt=F32):
            return ctx.enter_context(nc.psum_tensor(name, shape, dt))

        def sem(name):
            return ctx.enter_context(nc.semaphore(name))

        w_qk = sb("w_qk", [P, KD, NG, 2 * GC])
        w_v = sb("w_v", [P, KD, D])
        w_o = sb("w_o", [P, KD, D])
        w_e = sb("w_e", [P, KE, 2 * D])
        nw_col = sb("nw_col", [P, KD])
        nb_col = sb("nb_col", [P, KD])
        nb_wide = sb("nb_wide", [P, KD, P])
        sbw_col = sb("sbw_col", [P, KD])
        sbb_col = sb("sbb_col", [P, KD])
        eb_col = sb("eb_col", [P, 2 * KD])
        qkb_col = sb("qkb_col", [P, NG])
        vb_row = sb("vb_row", [P, D])
        ob_row = sb("ob_row", [P, D])
        ident = sb("ident", [P, P])
        exponent = sb("exponent", [P, CH])
        cond_in = sb("cond_in", [B, TE])
        cond_tanh = sb("cond_tanh", [B, TE])
        cond_silu = sb("cond_silu", [B, TE])
        cond_t = sb("cond_t", [P, KE, B])
        emb_t = sb("emb_t", [P, 2 * KD, B])
        mod_a = sb("mod_a", [P, 2, KD, B])
        mod_b = sb("mod_b", [P, 2, KD, B])
        mod_now = sb("mod_now", [P, 4, KD])
        mask_in = sb("mask_in", [B, T])
        mask_bias = sb("mask_bias", [B, T])
        mask_rest = sb("mask_rest", [B, 2, T])
        mask_parts = sb("mask_parts", [B, PARTS, T], BF16)
        mask_col = sb("mask_col", [P, CH, B])
        mask_now = sb("mask_now", [P, CH])
        x_in = sb("x_in", [P, CH, D])
        spacer = sb("spacer", [P, 1])
        x_stats = sb("x_stats", [P, CH, 6])
        x_mv = sb("x_mv", [P, CH, 2])
        x_negmean = sb("x_negmean", [P, CH])
        x_vareps = sb("x_vareps", [P, CH])
        x_rstd = sb("x_rstd", [P, CH])
        x_norm = sb("x_norm", [P, CH, D])
        x_norm_t = sb("x_norm_t", [P, KD, T])
        qk_full = sb("qk_full", [P, T])
        qk_rest = sb("qk_rest", [P, T])
        qk_parts = sb("qk_parts", [P, PARTS, T], BF16)
        q_rows = sb("q_rows", [P, NG, GH, T], BF16)
        k_rows = sb("k_rows", [P, NG, GH, T], BF16)
        negmax = sb("negmax", [P, 2, GH * CH])
        max_parts = sb("max_parts", [GH * CH, 2, 2, P], BF16)
        v_plain = sb("v_plain", [P, CH, D])
        v_biased = sb("v_biased", [P, CH, GC])
        v_rows = sb("v_rows", [P, CH, HEADS, VW])
        probs = sb("probs", [P, P_SLOTS, GH, T])
        y_t = sb("y_t", [P, T])
        y_recip = sb("y_recip", [P, CH, GH])
        y = sb("y", [P, CH, D])
        y_stats = sb("y_stats", [P, CH, 6])
        y_mv = sb("y_mv", [P, CH, 2])
        y_negmean = sb("y_negmean", [P, CH])
        y_vareps = sb("y_vareps", [P, CH])
        y_rstd = sb("y_rstd", [P, CH])
        y_norm = sb("y_norm", [P, CH, D])
        h_tanh = sb("h_tanh", [P, KD, T])
        h_lin = sb("h_lin", [P, KD, T])
        h_t = sb("h_t", [P, KD, T])
        x_res = sb("x_res", [P, CH, D])
        out_sb = sb("out_sb", [P, CH, D])
        st_ps = [psum(f"st_ps{i}", [P, T]) for i in range(ST_BANKS)]
        mx_ps = [psum(f"mx_ps{i}", [P, T]) for i in range(MX_BANKS)]
        pv_ps = psum("pv_ps", [P, T])
        job_ps = [psum(f"job_ps{i}", [P, T]) for i in range(2)]
        qk_dram = nc.dram_tensor("qk_dram", (NG, 2, PARTS, HD, GH, T), BF16, kind="Internal").ap()
        mask_dram = nc.dram_tensor("mask_dram", (B, PARTS, T), BF16, kind="Internal").ap()

        x_loaded = sem("x_loaded")
        res_loaded = sem("res_loaded")
        cond_loaded = sem("cond_loaded")
        mask_loaded = sem("mask_loaded")
        weights_loaded = sem("weights_loaded")
        mask_saved = sem("mask_saved")
        parts_saved = [sem(f"parts_saved{i}") for i in range(PARTS)]
        rows_filled = [sem(f"rows_filled{i}") for i in range(NG)]
        max_filled = [sem(f"max_filled{i}") for i in range(NG)]
        out_saved = sem("out_saved")
        consts_ready = sem("consts_ready")
        rows_preset = sem("rows_preset")
        wide_ready = sem("wide_ready")
        tanh_ready = sem("tanh_ready")
        bias_summed = sem("bias_summed")
        mask_turned = sem("mask_turned")
        silu_ready = sem("silu_ready")
        cond_turned = sem("cond_turned")
        cond_ready = sem("cond_ready")
        emb_ready = sem("emb_ready")
        weights_ready = sem("weights_ready")
        maskp_ready = sem("maskp_ready")
        setup_chain = sem("setup_chain")
        pool_chain = sem("pool_chain")
        split_chain = sem("split_chain")
        setup_done = sem("setup_done")
        max_ready = sem("max_ready")
        st_ready = sem("st_ready")
        pv_done = sem("pv_done")
        turned = {k: sem(f"{k}_done") for k in ("proj", "yturn", "cturn", "xturn", "hturn", "outp", "vproj")}
        max_done = sem("max_done")
        exp_done = sem("exp_done")
        part0_ready = sem("part0_ready")
        rest_ready = sem("rest_ready")
        part1_ready = sem("part1_ready")
        part2_ready = sem("part2_ready")
        max_split = sem("max_split")
        xt_ready = sem("xt_ready")
        v_plain_ready = sem("v_plain_ready")
        v_biased_ready = sem("v_biased_ready")
        v_ready = sem("v_ready")
        yt_ready = sem("yt_ready")
        recip_ready = sem("recip_ready")
        y_ready = sem("y_ready")
        bn_ready = sem("bn_ready")
        x_stat_ready = sem("x_stat_ready")
        x_rstd_ready = sem("x_rstd_ready")
        x_norm_ready = sem("x_norm_ready")
        y_stat_ready = sem("y_stat_ready")
        y_rstd_ready = sem("y_rstd_ready")
        y_norm_ready = sem("y_norm_ready")
        now_ready = sem("now_ready")
        mod_ready = sem("mod_ready")
        h_lin_ready = sem("h_lin_ready")
        h_ready = sem("h_ready")
        res_ready = sem("res_ready")
        out_ready = sem("out_ready")

        x_dram = x.rearrange("b (c p) f -> b p c f", p=P)
        out_dram = out.rearrange("b (c p) f -> b p c f", p=P)

        def batch_of(view, batch):
            return view[bass.ds(batch, 1)].rearrange("a p c f -> (a p) c f")

        def emptied(kind, i, batch):
            if kind == "proj":
                return part0_ready, NG * batch + i + 1
            if kind == "yturn":
                return y_ready, NG * batch + i + 1
            if kind == "cturn":
                return max_split, NG * batch + i + 1
            of = {"xturn": xt_ready, "vproj": v_plain_ready, "hturn": h_lin_ready, "outp": out_ready}[kind]
            return of, 2 * batch + i + 1

        def bank_freed(at, b):
            for back in range(at - 2, at - 2 * len(JOBS), -2):
                _, kind, i, db = JOBS[back % len(JOBS)]
                loop_b = b + back // len(JOBS)
                if isinstance(loop_b, int) and loop_b < -1:
                    return None
                if job_exists(kind, i, db, loop_b):
                    return emptied(kind, i, loop_b + db)
            return None

        def run(engine, body):
            for b in (-1, 0, 1):
                body(b)
            with engine.Fori(2, B - 1) as b:
                body(b)
            body(B - 1)
            body(B)

        block = ctx.enter_context(nc.Block())

        @block.tensor
        def _(pe):
            pe.wait_ge(weights_loaded, WEIGHT_DMAS * 16)
            pe.wait_ge(wide_ready, 1)
            for g in range(NG):
                for k in range(KD):
                    pe.matmul(st_ps[0][:, g:g + 1], w_qk[:, k, g, :], nb_col[:, k:k + 1],
                              start=(k == 0), stop=(k == KD - 1))
            for k in range(KD):
                mm = pe.matmul(st_ps[1][:, 0:D], nb_wide[:, k, :], w_v[:, k, :], start=(k == 0), stop=(k == KD - 1))
            mm.then_inc(bias_summed, 1)
            pe.wait_ge(consts_ready, 1)
            pe.wait_ge(mask_loaded, 16)
            for c in range(CH):
                mm = pe.transpose(mx_ps[1][:, c * B:(c + 1) * B], mask_in[:, c * P:(c + 1) * P], ident[0:B, 0:B])
            mm.then_inc(mask_turned, 1)
            pe.wait_ge(silu_ready, 1)
            for k in range(KE):
                mm = pe.transpose(st_ps[2][:, k * B:(k + 1) * B], cond_silu[:, k * P:(k + 1) * P], ident[0:B, 0:B])
            mm.then_inc(cond_turned, 1)
            pe.wait_ge(cond_ready, 1)
            for m in range(2 * KD):
                for k in range(KE):
                    mm = pe.matmul(mx_ps[0][:, m * B:(m + 1) * B], w_e[:, k, m * P:(m + 1) * P], cond_t[:, k, :],
                                   start=(k == 0), stop=(k == KE - 1))
            mm.then_inc(emb_ready, 1)
            pe.wait_ge(setup_done, 1)

            def max_unit(b, t, h):
                ahead = t + MAX_LEAD
                mb, step = (b, ahead) if ahead < STEPS else (b + 1, ahead - STEPS)
                if not exists(mb):
                    return
                g, c = step // CH, step % CH
                if c == 0 and h == 0:
                    pe.wait_ge(rows_filled[g], ROW_DMAS * 16 * (mb + 1))
                unit = UNITS * mb + GH * step + h
                wait(pe, max_done, unit - MX_BANKS + 1)
                pe.matmul(mx_ps[h % MX_BANKS][:, :], q_rows[0:ROWS_MASK, g, h, c * P:(c + 1) * P],
                          k_rows[0:ROWS_MASK, g, h, :], start=True, stop=True).then_inc(max_ready, 1)

            def st_unit(b, t, h):
                if not exists(b):
                    return
                g, c = t // CH, t % CH
                if c == 0 and h == 0:
                    pe.wait_ge(max_filled[g], 2 * 16 * (b + 1))
                u = GH * t + h
                before = u - ST_BANKS if u >= ST_BANKS else max(
                    v for v in range(UNITS) if v % ST_BANKS == u % ST_BANKS) - UNITS
                wait(pe, exp_done, UNITS * b + before + 1)
                pe.matmul(st_ps[u % ST_BANKS][:, :], k_rows[0:ROWS_ALL, g, h, c * P:(c + 1) * P],
                          q_rows[0:ROWS_ALL, g, h, :], start=True, stop=True).then_inc(st_ready, 1)

            def pv_step(b, t):
                b, t = (b, t - 1) if t else (b - 1, STEPS - 1)
                if not exists(b):
                    return
                g, c = t // CH, t % CH
                if c == 0:
                    pe.wait_ge(v_ready, NG * b + g + 1)
                    wait(pe, yt_ready, NG * b + g)
                pe.wait_ge(exp_done, UNITS * b + GH * (t + 1))
                for h in range(GH):
                    mm = pe.matmul(pv_ps[VW * h:VW * (h + 1), :], v_rows[:, c, g * GH + h, :], probs[:, t % P_SLOTS, h, :],
                                   start=(c == 0), stop=(c == CH - 1), tile_position=(0, VW * h), skip_group_check=True)
                mm.then_inc(pv_done, 1)

            def job(at, b):
                _, kind, i, db = JOBS[at]
                if not job_exists(kind, i, db, b):
                    return
                ps, d = job_ps[at % 2], b + db
                freed = bank_freed(at, b)
                if freed:
                    wait(pe, *freed)
                if kind == "proj":
                    pe.wait_ge(xt_ready, KD * (d + 1))
                    for k in range(KD):
                        mm = pe.matmul(ps[:, :], w_qk[:, k, i, :], x_norm_t[:, k, :], start=(k == 0), stop=(k == KD - 1))
                elif kind == "vproj":
                    pe.wait_ge(xt_ready, KD * (d + 1))
                    for c in range(2):
                        tok = (2 * i + c) * P
                        for k in range(KD):
                            mm = pe.matmul(ps[:, c * D:(c + 1) * D], x_norm_t[:, k, tok:tok + P], w_v[:, k, :],
                                           start=(k == 0), stop=(k == KD - 1))
                elif kind == "xturn":
                    pe.wait_ge(x_norm_ready, CH * (d + 1))
                    for c in range(CH):
                        mm = pe.transpose(ps[:, c * P:(c + 1) * P], x_norm[:, c, i * P:(i + 1) * P], ident[:, :])
                elif kind == "cturn":
                    pe.wait_ge(max_done, GH * CH * (NG * d + i + 1))
                    mm = pe.transpose(ps[0:GH * CH, 0:P], negmax[:, i % 2, :], ident[:, :])
                elif kind == "yturn":
                    pe.wait_ge(yt_ready, NG * d + i + 1)
                    for c in range(CH):
                        mm = pe.transpose(ps[:, c * P:(c + 1) * P], y_t[:, c * P:(c + 1) * P], ident[:, :])
                elif kind == "hturn":
                    pe.wait_ge(y_norm_ready, CH * (d + 1))
                    for c in range(CH):
                        mm = pe.transpose(ps[:, c * P:(c + 1) * P], y_norm[:, c, i * P:(i + 1) * P], ident[:, :])
                else:
                    pe.wait_ge(h_ready, KD * (d + 1))
                    for c in range(2):
                        tok = (2 * i + c) * P
                        for k in range(KD):
                            mm = pe.matmul(ps[:, c * D:(c + 1) * D], h_t[:, k, tok:tok + P], w_o[:, k, :],
                                           start=(k == 0), stop=(k == KD - 1))
                mm.then_inc(turned[kind], 1)

            def body(b):
                for t in range(STEPS):
                    jobs = [n for n in range(len(JOBS)) if JOBS[n][0] == t]
                    for h in range(GH):
                        if h == GH // 2:
                            pv_step(b, t)
                            for n in jobs:
                                if JOBS[n][1] == "cturn":
                                    job(n, b)
                        max_unit(b, t, h)
                        st_unit(b, t, h)
                    for n in jobs:
                        if JOBS[n][1] != "cturn":
                            job(n, b)

            run(pe, body)

        @block.scalar
        def _(act):
            act.wait_ge(cond_loaded, 16)
            act.activation(cond_tanh[:, :], cond_in[:, :], ACT.Tanh, scale=0.5).then_inc(tanh_ready, 1)
            act.wait_ge(setup_done, 1)

            def exp_unit(b, t, h):
                if not exists(b):
                    return
                u = GH * t + h
                if h == 0:
                    wait(act, pv_done, STEPS * b + t - P_SLOTS + 1)
                act.wait_ge(st_ready, UNITS * b + u + 1)
                act.activation(probs[:, t % P_SLOTS, h, :], st_ps[u % ST_BANKS][:, :], ACT.Exp).then_inc(exp_done, 1)

            def read_job(at, b):
                _, kind, i, db = JOBS[at]
                if not job_exists(kind, i, db, b):
                    return
                ps, d = job_ps[at % 2], b + db
                if kind == "proj":
                    act.wait_ge(turned["proj"], NG * d + i + 1)
                    wait(act, rest_ready, NG * d + i)
                    act.activation(qk_full[:, :], ps[:, :], ACT.Identity, bias=qkb_col[:, i:i + 1])
                    wait(act, parts_saved[0], 2 * 16 * (NG * d + i))
                    act.activation(qk_parts[:, 0, :], ps[:, :], ACT.Identity,
                                   bias=qkb_col[:, i:i + 1]).then_inc(part0_ready, 1)
                elif kind == "xturn":
                    act.wait_ge(turned["xturn"], KD * d + i + 1)
                    wait(act, turned["proj"], NG * d)
                    act.copy(x_norm_t[:, i, :], ps[:, :]).then_inc(xt_ready, 1)
                elif kind == "vproj":
                    act.wait_ge(turned["vproj"], 2 * d + i + 1)
                    wait(act, v_biased_ready, NG * d)
                    act.copy(v_plain[:, 2 * i:2 * i + 2, :], ps[:, :].rearrange("p (c f) -> p c f", f=D)
                             ).then_inc(v_plain_ready, 1)
                elif kind == "hturn":
                    act.wait_ge(turned["hturn"], KD * d + i + 1)
                    act.wait_ge(mod_ready, d + 1)
                    wait(act, h_ready, KD * d)
                    act.activation(h_tanh[:, i, :], ps[:, :], ACT.Tanh, bias=mod_now[:, 3, i:i + 1],
                                   scale=mod_now[:, 1, i:i + 1])
                    act.activation(h_lin[:, i, :], ps[:, :], ACT.Identity, bias=mod_now[:, 2, i:i + 1],
                                   scale=mod_now[:, 0, i:i + 1]).then_inc(h_lin_ready, 1)
                elif kind == "cturn":
                    g = i % NG
                    act.wait_ge(max_split, NG * d + i + 1)
                    for part in range(2):
                        act.dma_start(
                            q_rows[ROWS_MASK + part:ROWS_MASK + part + 1, g, :, :].rearrange(
                                "p h (c t) -> p (h c) t", t=P),
                            max_parts[:, i % 2, part:part + 1, :]).then_inc(max_filled[g], 16)

            def yt_copy(b, t):
                n = t // CH - 1
                b, g = (b, n) if n >= 0 else (b - 1, NG - 1)
                if not exists(b):
                    return
                act.wait_ge(pv_done, STEPS * b + CH * (g + 1))
                wait(act, turned["yturn"], NG * b + g)
                act.copy(y_t[:, :], pv_ps[:, :]).then_inc(yt_ready, 1)

            def body(b):
                for t in range(STEPS):
                    exp_unit(b, t, 0)
                    for n, j in enumerate(JOBS):
                        if j[0] == t - 1:
                            read_job(n, b)
                        elif t == 0 and j[0] == STEPS - 1:
                            if not isinstance(b, int) or b > -1:
                                read_job(n, b - 1)
                    for h in range(1, GH):
                        if t % CH == 0 and h == GH - 1:
                            yt_copy(b, t)
                        exp_unit(b, t, h)

            run(act, body)

        @block.vector
        def _(dve):
            dve.memset(q_rows[ROWS_PROD:P, :, :, :], 1.0).then_inc(rows_preset, 1)
            dve.memset(k_rows[ROWS_PROD:P, :, :, :], 1.0).then_inc(rows_preset, 1)
            dve.wait_ge(mask_loaded, 16)
            dve.tensor_scalar(mask_bias[:, :], mask_in[:, :], -1.0, MASKED, ALU.add, ALU.mult).then_inc(setup_chain, 1)
            dve.wait_ge(setup_chain, 1)
            dve.tensor_copy(mask_parts[:, 0, :], mask_bias[:, :]).then_inc(setup_chain, 1)
            dve.wait_ge(setup_chain, 2)
            dve.tensor_tensor(mask_rest[:, 0, :], mask_bias[:, :], mask_parts[:, 0, :], ALU.subtract).then_inc(setup_chain, 1)
            dve.wait_ge(setup_chain, 3)
            dve.tensor_copy(mask_parts[:, 1, :], mask_rest[:, 0, :]).then_inc(setup_chain, 1)
            dve.wait_ge(setup_chain, 4)
            dve.tensor_tensor(mask_rest[:, 1, :], mask_rest[:, 0, :], mask_parts[:, 1, :], ALU.subtract).then_inc(setup_chain, 1)
            dve.wait_ge(setup_chain, 5)
            dve.tensor_copy(mask_parts[:, 2, :], mask_rest[:, 1, :]).then_inc(maskp_ready, 1)
            dve.wait_ge(tanh_ready, 1)
            dve.scalar_tensor_tensor(cond_tanh[:, :], cond_tanh[:, :], 1.0, cond_in[:, :], ALU.add, ALU.mult
                                     ).then_inc(setup_chain, 1)
            dve.wait_ge(setup_chain, 6)
            dve.tensor_scalar(cond_silu[:, :], cond_tanh[:, :], 0.5, None, ALU.mult).then_inc(silu_ready, 1)
            dve.wait_ge(weights_loaded, WEIGHT_DMAS * 16)
            dve.wait_ge(bias_summed, 1)
            dve.tensor_tensor(qkb_col[:, :], qkb_col[:, :], st_ps[0][:, 0:NG], ALU.add)
            dve.tensor_tensor(vb_row[:, :], vb_row[:, :], st_ps[1][:, 0:D], ALU.add)
            for k in range(KD):
                dve.tensor_scalar(w_qk[:, k, :, :], w_qk[:, k, :, :], nw_col[:, k:k + 1], None, ALU.mult)
                dve.tensor_scalar(w_v[:, k, :], w_v[:, k, :], nw_col[:, k:k + 1], None, ALU.mult)
            dve.tensor_scalar(w_o[:, :, :], w_o[:, :, :], 0.5, None, ALU.mult)
            dve.wait_ge(mask_turned, 1)
            dve.tensor_copy(mask_col[:, :, :], mx_ps[1][:, 0:CH * B].rearrange("p (c b) -> p c b", b=B))
            dve.wait_ge(cond_turned, 1)
            dve.tensor_copy(cond_t[:, :, :], st_ps[2][:, 0:KE * B].rearrange("p (k b) -> p k b", b=B)).then_inc(cond_ready, 1)
            dve.wait_ge(emb_ready, 1)
            for m in range(2 * KD):
                dve.tensor_scalar(emb_t[:, m, :], mx_ps[0][:, m * B:(m + 1) * B], eb_col[:, m:m + 1],
                                  1.0 if m < KD else 0.0, ALU.add, ALU.add).then_inc(setup_chain, 1)
            dve.wait_ge(setup_chain, 6 + 2 * KD)
            for k in range(KD):
                dve.tensor_scalar(mod_a[:, 0, k, :], emb_t[:, k, :], sbw_col[:, k:k + 1], None, ALU.mult)
                dve.scalar_tensor_tensor(mod_b[:, 0, k, :], emb_t[:, k, :], sbb_col[:, k:k + 1], emb_t[:, KD + k, :],
                                         ALU.mult, ALU.add).then_inc(setup_chain, 1)
            dve.wait_ge(setup_chain, 6 + 3 * KD)
            dve.tensor_scalar(mod_a[:, 1, :, :], mod_a[:, 0, :, :], 0.5, None, ALU.mult)
            dve.tensor_scalar(mod_b[:, 1, :, :], mod_b[:, 0, :, :], 0.5, None, ALU.mult).then_inc(setup_done, 1)

            def max_unit(b, t, h):
                ahead = t + MAX_LEAD
                mb, step = (b, ahead) if ahead < STEPS else (b + 1, ahead - STEPS)
                if not exists(mb):
                    return
                g, c = step // CH, step % CH
                if c == 0 and h == 0:
                    wait(dve, turned["cturn"], NG * mb + g - 1)
                dve.wait_ge(max_ready, UNITS * mb + GH * step + h + 1)
                dve.tensor_reduce(negmax[:, g % 2, h * CH + c:h * CH + c + 1], mx_ps[h % MX_BANKS][:, :],
                                  AXIS_X, ALU.max, negate=True).then_inc(max_done, 1)

            def stats(src, raw, mv, negmean, vareps, ready, nth):
                for c in range(CH):
                    dve.bn_stats(raw[:, c, :], src[:, c, :]).then_inc(bn_ready, 1)
                dve.wait_ge(bn_ready, 2 * CH * nth + CH)
                dve.memset(spacer[:, :], 0.0)
                for c in range(CH):
                    dve.bn_aggr(mv[:, c, :], raw[:, c, :]).then_inc(bn_ready, 1)
                dve.wait_ge(bn_ready, 2 * CH * (nth + 1))
                dve.tensor_scalar(negmean[:, :], mv[:, :, 0], -1.0, None, ALU.mult)
                dve.tensor_scalar(vareps[:, :], mv[:, :, 1], EPS, None, ALU.add).then_inc(ready, 1)

            def split_max(at, b):
                _, kind, i, db = JOBS[at]
                if not job_exists(kind, i, db, b):
                    return
                ps, n = job_ps[at % 2], NG * b + i
                dve.wait_ge(turned["cturn"], n + 1)
                if not isinstance(b, int) or n >= 2:
                    lap, slot = (b, i - 2) if i >= 2 else (b - 1, i - 2 + NG)
                    dve.wait_ge(max_filled[slot], 2 * 16 * (lap + 1))
                dve.tensor_copy(max_parts[:, i % 2, 0, :], ps[0:GH * CH, 0:P]).then_inc(split_chain, 1)
                dve.wait_ge(split_chain, n + 1)
                dve.tensor_tensor(max_parts[:, i % 2, 1, :], ps[0:GH * CH, 0:P], max_parts[:, i % 2, 0, :],
                                  ALU.subtract).then_inc(max_split, 1)

            def read_job(at, b):
                _, kind, i, db = JOBS[at]
                if not job_exists(kind, i, db, b):
                    return
                ps, d = job_ps[at % 2], b + db
                if kind == "yturn":
                    by_head = ps[:, :].rearrange("p (c h w) -> p c h w", h=GH, w=VW)
                    dve.wait_ge(turned["yturn"], NG * d + i + 1)
                    wait(dve, y_ready, NG * d + i)
                    dve.reciprocal(y_recip[:, :, :], by_head[:, :, :, HD]).then_inc(recip_ready, 1)
                    dve.wait_ge(recip_ready, NG * d + i + 1)
                    wait(dve, y_norm_ready, CH * d)
                    dve.tensor_tensor(y[:, :, i * GC:(i + 1) * GC].rearrange("p c (h l) -> p c h l", l=HD),
                                      by_head[:, :, :, 0:HD],
                                      y_recip[:, :, :].unsqueeze(3).broadcast_to((P, CH, GH, HD)),
                                      ALU.mult).then_inc(y_ready, 1)
                elif kind == "outp":
                    dve.wait_ge(turned["outp"], 2 * d + i + 1)
                    dve.wait_ge(res_ready, d + 1)
                    wait(dve, out_saved, 2 * 16 * d)
                    dve.tensor_tensor(out_sb[:, 2 * i:2 * i + 2, :], ps[:, :].rearrange("p (c f) -> p c f", f=D),
                                      x_res[:, 2 * i:2 * i + 2, :], ALU.add).then_inc(out_ready, 1)

            def late_job(at, b):
                _, kind, i, db = JOBS[at]
                if not job_exists(kind, i, db, b):
                    return
                d = b + db
                if kind == "proj":
                    n = NG * d + i
                    dve.wait_ge(rest_ready, n + 1)
                    wait(dve, parts_saved[1], 2 * 16 * n)
                    dve.tensor_copy(qk_parts[:, 1, :], qk_rest[:, :]).then_inc(part1_ready, 1)
                elif kind == "hturn":
                    dve.wait_ge(h_lin_ready, KD * d + i + 1)
                    wait(dve, turned["outp"], 2 * d)
                    dve.scalar_tensor_tensor(h_t[:, i, :], h_tanh[:, i, :], 1.0, h_lin[:, i, :], ALU.add, ALU.mult
                                             ).then_inc(h_ready, 1)

            def body(b):
                for t in range(STEPS):
                    max_unit(b, t, 0)
                    for n, j in enumerate(JOBS):
                        if j[0] == t - 1:
                            read_job(n, b)
                    for h in range(1, GH):
                        max_unit(b, t, h)
                    for n, j in enumerate(JOBS):
                        if j[0] == t and j[1] == "cturn":
                            split_max(n, b)
                        elif j[0] == t - 1:
                            late_job(n, b)
                    if t == 0 and exists(b + 1):
                        dve.wait_ge(x_loaded, 16 * (b + 2))
                        wait(dve, x_norm_ready, CH * (b + 1))
                        stats(x_in, x_stats, x_mv, x_negmean, x_vareps, x_stat_ready, nth_stats(b, 0))
                    if t == 2 and exists(b - 1):
                        dve.wait_ge(y_ready, NG * b)
                        wait(dve, y_norm_ready, CH * (b - 1))
                        stats(y, y_stats, y_mv, y_negmean, y_vareps, y_stat_ready, nth_stats(b, 1))

            def nth_stats(b, which):
                if not isinstance(b, int):
                    return 2 * b + which
                return sum(exists(i + 1) + exists(i - 1) for i in range(-1, b)) + (which if exists(b + 1) else 0)

            run(dve, body)

        @block.gpsimd
        def _(pool):
            pool.memset(ident[:, :], 1.0).then_inc(pool_chain, 1)
            pool.wait_ge(pool_chain, 1)
            pool.affine_select(ident[:, :], ident[:, :], pattern=[[-1, P]], compare_op=ALU.is_equal, fill=0.0,
                               base=0, channel_multiplier=1).then_inc(consts_ready, 1)
            pool.memset(exponent[:, :], -0.5)
            pool.memset(v_rows[:, :, :, :], 0.0).then_inc(pool_chain, 1)
            pool.wait_ge(pool_chain, 2)
            pool.memset(v_rows[:, :, :, HD:HD + 1], 1.0).then_inc(pool_chain, 1)
            pool.wait_ge(weights_loaded, WEIGHT_DMAS * 16)
            pool.tensor_copy(nb_wide[:, :, :], nb_col[:, :].unsqueeze(2).broadcast_to((P, KD, P))).then_inc(wide_ready, 1)
            pool.wait_ge(setup_done, 1)
            pool.wait_ge(pool_chain, 3)

            def norm(src, dst, negmean, vareps, rstd, stat_ready, rstd_ready, norm_ready, d):
                pool.wait_ge(stat_ready, d + 1)
                pool.tensor_tensor(rstd[:, :], vareps[:, :], exponent[:, :], ALU.pow).then_inc(rstd_ready, 1)
                wait_apart(pool, setup_done, rstd_ready, d + 1)
                for c in range(CH):
                    pool.tensor_scalar(dst[:, c, :], src[:, c, :], negmean[:, c:c + 1], rstd[:, c:c + 1],
                                       ALU.add, ALU.mult).then_inc(norm_ready, 1)

            def take_rest(b, i, db):
                if not exists(b + db):
                    return
                n = NG * (b + db) + i
                pool.wait_ge(part0_ready, n + 1)
                wait(pool, part1_ready, n)
                wait(pool, part2_ready, n)
                pool.tensor_tensor(qk_rest[:, :], qk_full[:, :], qk_parts[:, 0, :], ALU.subtract).then_inc(rest_ready, 1)

            def take_part2(b, i, db):
                if not exists(b + db):
                    return
                n = NG * (b + db) + i
                pool.wait_ge(part1_ready, n + 1)
                wait(pool, parts_saved[2], 2 * 16 * n)
                pool.tensor_tensor(qk_parts[:, 2, :], qk_rest[:, :], qk_parts[:, 1, :], ALU.subtract).then_inc(part2_ready, 1)

            def values(b, g):
                if not exists(b):
                    return
                n = NG * b + g
                pool.wait_ge(v_plain_ready, 2 * (b + 1))
                wait(pool, v_ready, n)
                pool.tensor_tensor(v_biased[:, :, :], v_plain[:, :, g * GC:(g + 1) * GC],
                                   vb_row[:, g * GC:(g + 1) * GC].unsqueeze(1).broadcast_to((P, CH, GC)),
                                   ALU.add).then_inc(v_biased_ready, 1)
                pool.wait_ge(v_biased_ready, n + 1)
                wait(pool, pv_done, STEPS * (b - 1) + CH * (g + 1))
                pool.tensor_tensor(v_rows[:, :, g * GH:(g + 1) * GH, 0:HD],
                                   v_biased[:, :, :].rearrange("p c (h l) -> p c h l", l=HD),
                                   mask_now[:, :].unsqueeze(2).unsqueeze(3).broadcast_to((P, CH, GH, HD)),
                                   ALU.mult).then_inc(v_ready, 1)

            def body(b):
                if exists(b):
                    wait(pool, v_ready, NG * b)
                    pool.tensor_copy(mask_now[:, :], mask_col[:, :, bass.ds(b, 1)].rearrange("p c b -> p (c b)")
                                     ).then_inc(now_ready, 1)
                    pool.wait_ge(now_ready, b + 1)
                values(b, 0)
                take_rest(b, 3, 0)
                if exists(b + 1):
                    wait(pool, turned["xturn"], KD * (b + 1))
                    norm(x_in, x_norm, x_negmean, x_vareps, x_rstd, x_stat_ready, x_rstd_ready, x_norm_ready, b + 1)
                take_part2(b, 3, 0)
                if exists(b - 1):
                    wait(pool, turned["hturn"], KD * (b - 1))
                    norm(y, y_norm, y_negmean, y_vareps, y_rstd, y_stat_ready, y_rstd_ready, y_norm_ready, b - 1)
                    wait(pool, h_lin_ready, KD * (b - 1))
                    for n, src in enumerate((mod_a, mod_b)):
                        mm = pool.tensor_copy(mod_now[:, 2 * n:2 * n + 2, :],
                                              src[:, :, :, bass.ds(b - 1, 1)].rearrange("p a k b -> p a (k b)"))
                    mm.then_inc(mod_ready, 1)
                values(b, 1)
                take_rest(b, 0, 1)
                take_part2(b, 0, 1)
                if exists(b - 1):
                    pool.wait_ge(res_loaded, 16 * b)
                    pool.tensor_tensor(x_res[:, :, :], x_res[:, :, :],
                                       ob_row[:, :].unsqueeze(1).broadcast_to((P, CH, D)), ALU.add).then_inc(res_ready, 1)
                for g in (1, 2):
                    values(b, g + 1)
                    take_rest(b, g, 1)
                    take_part2(b, g, 1)

            run(pool, body)

        @block.sync
        def _(sp):
            sp.dma_start(x_in[:, :, :], batch_of(x_dram, 0)).then_inc(x_loaded, 16)
            sp.dma_start(mask_in[:, :], mask[:, :]).then_inc(mask_loaded, 16)
            sp.dma_start(cond_in[:, :], cond[:, :]).then_inc(cond_loaded, 16)
            with nc.allow_non_contiguous_dma(reason="small vectors, once"):
                loads = []
                for k in range(KD):
                    for n, w in enumerate((q_w, k_w)):
                        loads.append((w_qk[:, k, :, n * GC:(n + 1) * GC],
                                      w[k * P:(k + 1) * P, :].rearrange("p (g c) -> p g c", c=GC)))
                for dst, src in ((w_v, v_w), (w_o, out_w), (w_e, emb_w)):
                    loads.append((dst[:, :, :], src.rearrange("(k p) n -> p k n", p=P)))
                for dst, src in ((nw_col, norm_w), (nb_col, norm_b), (sbw_col, sb_w), (sbb_col, sb_b), (eb_col, emb_b)):
                    loads.append((dst[:, :], src.rearrange("(k p) -> p k", p=P)))
                for n, src in enumerate((q_b, k_b)):
                    loads.append((qkb_col[n * GC:(n + 1) * GC, :], src.rearrange("(g c) -> c g", c=GC)))
                for dst, src in ((vb_row, v_b), (ob_row, out_b)):
                    loads.append((dst[:, :], src.rearrange("(a n) -> a n", a=1).broadcast_to((P, D))))
                assert len(loads) == WEIGHT_DMAS
                for dst, src in loads:
                    sp.dma_start(dst, src).then_inc(weights_loaded, 16)
            sp.wait_ge(maskp_ready, 1)
            sp.dma_start(mask_dram[:, :, :], mask_parts[:, :, :]).then_inc(mask_saved, 16)
            sp.wait_ge(mask_saved, 16)
            sp.wait_ge(rows_preset, 2)

            def spread(b, i, db):
                d = b + db
                if not exists(d):
                    return
                n = NG * d + i
                for part, ready in enumerate((part0_ready, part1_ready, part2_ready)):
                    sp.wait_ge(ready, n + 1)
                    for m in range(2):
                        sp.dma_start(qk_dram[i, m, part].rearrange("l h t -> h l t"),
                                     qk_parts[m * GC:(m + 1) * GC, part, :]).then_inc(parts_saved[part], 16)
                sp.dma_start(k_rows[ROWS_PROD:ROWS_MASK, i, :, :],
                             mask_dram[bass.ds(d, 1)].rearrange("a s t -> (a s) t").unsqueeze(1).broadcast_to(
                                 (PARTS, GH, T))).then_inc(rows_filled[i], 16)
                q_src, k_src = (qk_dram[i, m].rearrange("s l h t -> s l (h t)") for m in range(2))
                for part in range(PARTS):
                    sp.wait_ge(parts_saved[part], 2 * 16 * (n + 1))
                    first, count = (0, 3, 5)[part], PARTS - part
                    sp.dma_start(k_rows[first * HD:(first + count) * HD, i, :, :].rearrange("p h t -> p (h t)"),
                                 k_src[part:part + 1].broadcast_to((count, HD, GH * T))).then_inc(rows_filled[i], 16)
                for first, count in ((0, 3), (3, 2), (5, 1)):
                    sp.dma_start(q_rows[first * HD:(first + count) * HD, i, :, :].rearrange("p h t -> p (h t)"),
                                 q_src[0:count]).then_inc(rows_filled[i], 16)

            def body(b):
                if exists(b + 1):
                    wait_apart(sp, maskp_ready, x_norm_ready, CH * (b + 1))
                    if not isinstance(b, int) or b >= 0:
                        sp.dma_start(x_in[:, :, :], batch_of(x_dram, b + 1)).then_inc(x_loaded, 16)
                spread(b, 3, 0)
                spread(b, 0, 1)
                spread(b, 1, 1)
                if exists(b - 1):
                    for i in range(2):
                        wait_apart(sp, maskp_ready, out_ready, 2 * (b - 1) + i + 1)
                        sp.dma_start(batch_of(out_dram, b - 1)[:, 2 * i:2 * i + 2, :], out_sb[:, 2 * i:2 * i + 2, :]
                                     ).then_inc(out_saved, 16)
                if exists(b):
                    sp.dma_start(x_res[:, :, :], batch_of(x_dram, b)).then_inc(res_loaded, 16)
                spread(b, 2, 1)

            run(sp, body)
            sp.wait_ge(out_saved, 2 * 16 * B)


WEIGHT_DMAS = 2 * KD + 3 + 5 + 2 + 2
ROW_DMAS = 7

_INS = ["x", "cond_2048", "mask_BxS_ff1", "L0_cond_norm_w", "L0_cond_norm_b", "L0_cond_q_w", "L0_cond_q_b",
        "L0_cond_k_w", "L0_cond_k_b", "L0_cond_v_w", "L0_cond_v_b", "L0_cond_emb_w", "L0_cond_emb_b",
        "L0_cond_sb_norm_w", "L0_cond_sb_norm_b", "L0_cond_out_w", "L0_cond_out_b"]


def kernel(**inputs):
    import numpy as _np
    import concourse.bacc as _bacc
    from concourse import mybir as _mybir
    from concourse.bass_utils import run_bass_kernel_spmd as _run

    nc = _bacc.Bacc("TRN2", target_bir_lowering=False, num_devices=1)
    arrays, args = {}, []
    for name in _INS:
        a = _np.ascontiguousarray(inputs[name])
        arrays[f"in_{name}"] = a
        args.append(nc.dram_tensor(f"in_{name}", a.shape, _mybir.dt.from_np(a.dtype), kind="ExternalInput").ap())
    args.append(nc.dram_tensor("out_0", (B, T, D), F32, kind="ExternalOutput").ap())
    attention_layer(nc, *args)
    r = _run(nc, [arrays], core_ids=[0])
    return r.results[0]["out_0"]
```

```python
from contextlib import ExitStack

import concourse.bass as bass
from concourse import mybir

F32 = mybir.dt.float32
BF16 = mybir.dt.bfloat16
ALU = mybir.AluOpType
ACT = mybir.ActivationFunctionType
AXIS_X = mybir.AxisListType.X

P = 128
B, T, D = 8, 512, 256
HEADS = 16
HD = D // HEADS
TE = 512
EPS = 1e-5
MASKED = 1000000.0
CH = T // P
KD = D // P
KE = TE // P
GH = 4
NG = HEADS // GH
GC = GH * HD
STEPS = NG * CH
UNITS = STEPS * GH
MAX_LEAD = 7
P_SLOTS = 4
ST_BANKS = 2
MX_BANKS = 3
JOB_BANKS = 2
PARTS = 3
ROWS_PROD = 6 * HD
ROWS_MASK = ROWS_PROD + PARTS
ROWS_ALL = ROWS_MASK + 2
VW = 32

TWO_ONES = 1.0 + 0x3F80 / 2 ** 23

MID, END = range(2)
JOBS = [
    (0, END, "proj", 3, 0), (1, MID, "cturn", 1, 0), (2, MID, "yturn", 3, -1), (3, MID, "xturn", 0, 1),
    (3, END, "xturn", 1, 1), (4, END, "proj", 0, 1), (5, MID, "cturn", 2, 0), (5, END, "vproj", 0, 1),
    (6, MID, "yturn", 0, 0), (6, END, "hturn", 0, -1), (7, MID, "vproj", 1, 1), (7, END, "hturn", 1, -1),
    (8, END, "proj", 1, 1), (9, MID, "cturn", 3, 0), (10, MID, "yturn", 1, 0), (10, END, "outp", 0, -1),
    (12, END, "proj", 2, 1), (13, MID, "cturn", 4, 0), (14, MID, "yturn", 2, 0), (14, END, "outp", 1, -1),
]


def jobs_at(step, place):
    return [n for n, j in enumerate(JOBS) if j[:2] == (step, place)]


def bank_of(unit, banks):
    return unit % banks if unit < UNITS - 1 else 1


def bank_before(unit, banks):
    return next(v for v in range(unit - 1, unit - UNITS, -1) if bank_of(v % UNITS, banks) == bank_of(unit, banks))


def exists(batch):
    return not isinstance(batch, int) or 0 <= batch < B


def job_exists(kind, i, db, b):
    if kind == "cturn" and i == NG:
        return exists(b + 1)
    return exists(b + db)


def wait(engine, semaphore, count):
    if not isinstance(count, int) or count > 0:
        engine.wait_ge(semaphore, count)


def wait_apart(engine, met, semaphore, count):
    if not isinstance(count, int):
        engine.wait_ge(met, 1)
    wait(engine, semaphore, count)


def attention_layer(nc, x, cond, mask, norm_w, norm_b, q_w, q_b, k_w, k_b, v_w, v_b,
                    emb_w, emb_b, sb_w, sb_b, out_w, out_b, out):
    with ExitStack() as ctx:
        def sb(name, shape, dt=F32):
            return ctx.enter_context(nc.sbuf_tensor(name, shape, dt))

        def psum(name, shape, dt=F32):
            return ctx.enter_context(nc.psum_tensor(name, shape, dt))

        def sem(name):
            return ctx.enter_context(nc.semaphore(name))

        w_qk = sb("w_qk", [P, KD, NG, 2 * GC])
        w_v = sb("w_v", [P, KD, D])
        w_o = sb("w_o", [P, KD, D])
        w_e = sb("w_e", [P, KE, 2 * D])
        nw_col = sb("nw_col", [P, KD])
        nb_col = sb("nb_col", [P, KD])
        sbw_col = sb("sbw_col", [P, KD])
        sbb_col = sb("sbb_col", [P, KD])
        eb_col = sb("eb_col", [P, 2 * KD])
        qkb_col = sb("qkb_col", [P, NG])
        vb_row = sb("vb_row", [P, D])
        ob_row = sb("ob_row", [P, D])
        ident = sb("ident", [P, P])
        exponent = sb("exponent", [P, CH])
        cond_in = sb("cond_in", [B, TE])
        cond_tanh = sb("cond_tanh", [B, TE])
        cond_silu = sb("cond_silu", [B, TE])
        cond_t = sb("cond_t", [P, KE, B])
        emb_t = sb("emb_t", [P, 2 * KD, B])
        mod_full = sb("mod_full", [P, 2, KD, B])
        mod_half = sb("mod_half", [P, 2, KD, B])
        mod_now = sb("mod_now", [P, 2, KD])
        mask_in = sb("mask_in", [B, T])
        mask_bias = sb("mask_bias", [B, T])
        mask_rest = sb("mask_rest", [B, 2, T])
        mask_parts = sb("mask_parts", [B, PARTS, T], BF16)
        mask_col = sb("mask_col", [P, CH, B])
        mask_now = sb("mask_now", [P, CH])
        x_in = sb("x_in", [P, CH, D])
        spacer = sb("spacer", [P, 1])
        x_stats = sb("x_stats", [P, CH, 6])
        x_mv = sb("x_mv", [P, CH, 2])
        x_negmean = sb("x_negmean", [P, CH])
        x_vareps = sb("x_vareps", [P, CH])
        x_rstd = sb("x_rstd", [P, CH])
        x_norm = sb("x_norm", [P, CH, D])
        x_norm_t = sb("x_norm_t", [P, KD, T])
        qk_full = sb("qk_full", [P, T])
        qk_rest = sb("qk_rest", [P, T])
        qk_parts = sb("qk_parts", [P, PARTS, T], BF16)
        q_rows = sb("q_rows", [P, NG, GH, T], BF16)
        k_rows = sb("k_rows", [P, NG, GH, T], BF16)
        negmax = sb("negmax", [P, 2, GH * CH])
        max_parts = sb("max_parts", [GH * CH, 2, 2, P], BF16)
        v_plain = sb("v_plain", [P, CH, D])
        v_biased = sb("v_biased", [P, CH, GC])
        v_rows = sb("v_rows", [P, CH, HEADS, VW])
        probs = sb("probs", [P, P_SLOTS, GH, T])
        y_t = sb("y_t", [P, T])
        y_recip = sb("y_recip", [P, CH, GH])
        y = sb("y", [P, CH, D])
        y_stats = sb("y_stats", [P, CH, 6])
        y_mv = sb("y_mv", [P, CH, 2])
        y_negmean = sb("y_negmean", [P, CH])
        y_vareps = sb("y_vareps", [P, CH])
        y_rstd = sb("y_rstd", [P, CH])
        y_norm = sb("y_norm", [P, CH, D])
        h_tanh = sb("h_tanh", [P, KD, T])
        h_lin = sb("h_lin", [P, KD, T])
        h_t = sb("h_t", [P, KD, T])
        x_res = sb("x_res", [P, CH, D])
        out_sb = sb("out_sb", [P, CH, D])
        st_ps = [psum(f"st_ps{i}", [P, T]) for i in range(ST_BANKS)]
        mx_ps = [psum(f"mx_ps{i}", [P, T]) for i in range(MX_BANKS)]
        pv_ps = psum("pv_ps", [P, T])
        job_ps = [psum(f"job_ps{i}", [P, T]) for i in range(JOB_BANKS)]
        qk_dram = nc.dram_tensor("qk_dram", (NG, PARTS, HD, 2 * GH, T), BF16, kind="Internal").ap()
        mask_dram = nc.dram_tensor("mask_dram", (B, PARTS, T), BF16, kind="Internal").ap()

        x_loaded = sem("x_loaded")
        res_loaded = sem("res_loaded")
        cond_loaded = sem("cond_loaded")
        mask_loaded = sem("mask_loaded")
        norm_loaded = sem("norm_loaded")
        weights_loaded = sem("weights_loaded")
        mask_saved = sem("mask_saved")
        parts_saved = [sem(f"parts_saved{i}") for i in range(PARTS)]
        rows_filled = [sem(f"rows_filled{i}") for i in range(NG)]
        max_filled = [sem(f"max_filled{i}") for i in range(NG)]
        out_saved = sem("out_saved")
        consts_ready = sem("consts_ready")
        q_preset = sem("q_preset")
        k_preset = sem("k_preset")
        tanh_ready = sem("tanh_ready")
        mask_turned = sem("mask_turned")
        mask_col_ready = sem("mask_col_ready")
        silu_ready = sem("silu_ready")
        cond_turned = sem("cond_turned")
        cond_ready = sem("cond_ready")
        emb_ready = sem("emb_ready")
        emb_loaded = sem("emb_loaded")
        maskp_ready = sem("maskp_ready")
        setup_chain = sem("setup_chain")
        pool_chain = sem("pool_chain")
        split_chain = sem("split_chain")
        setup_done = sem("setup_done")
        max_ready = sem("max_ready")
        st_ready = sem("st_ready")
        pv_done = sem("pv_done")
        turned = {k: sem(f"{k}_done") for k in ("proj", "yturn", "cturn", "xturn", "hturn", "outp", "vproj")}
        max_done = sem("max_done")
        exp_done = sem("exp_done")
        part0_ready = sem("part0_ready")
        rest_ready = sem("rest_ready")
        part1_ready = sem("part1_ready")
        part2_ready = sem("part2_ready")
        max_split = sem("max_split")
        xt_ready = sem("xt_ready")
        v_plain_ready = sem("v_plain_ready")
        v_biased_ready = sem("v_biased_ready")
        v_ready = sem("v_ready")
        yt_ready = sem("yt_ready")
        recip_ready = sem("recip_ready")
        y_ready = sem("y_ready")
        bn_ready = sem("bn_ready")
        x_stat_ready = sem("x_stat_ready")
        x_rstd_ready = sem("x_rstd_ready")
        x_norm_ready = sem("x_norm_ready")
        y_stat_ready = sem("y_stat_ready")
        y_rstd_ready = sem("y_rstd_ready")
        y_norm_ready = sem("y_norm_ready")
        now_ready = sem("now_ready")
        mod_ready = sem("mod_ready")
        h_lin_ready = sem("h_lin_ready")
        h_ready = sem("h_ready")
        res_ready = sem("res_ready")
        out_ready = sem("out_ready")

        x_dram = x.rearrange("b (c p) f -> b p c f", p=P)
        out_dram = out.rearrange("b (c p) f -> b p c f", p=P)

        def batch_of(view, batch):
            return view[bass.ds(batch, 1)].rearrange("a p c f -> (a p) c f")

        def emptied(kind, i, batch):
            if kind == "proj":
                return part0_ready, NG * batch + i + 1
            if kind == "yturn":
                return y_ready, NG * batch + i + 1
            if kind == "cturn":
                return max_split, NG * batch + i + 1
            of = {"xturn": xt_ready, "vproj": v_plain_ready, "hturn": h_lin_ready, "outp": out_ready}[kind]
            return of, 2 * batch + i + 1

        def bank_freed(at, b):
            for back in range(at - JOB_BANKS, at - 2 * len(JOBS), -JOB_BANKS):
                _, _, kind, i, db = JOBS[back % len(JOBS)]
                loop_b = b + back // len(JOBS)
                if isinstance(loop_b, int) and loop_b < -1:
                    return None
                if job_exists(kind, i, db, loop_b):
                    return emptied(kind, i, loop_b + db)
            return None

        def run(engine, body, stop=B - 1):
            for b in (-1, 0, 1):
                body(b)
            with engine.Fori(2, stop) as b:
                body(b)
            for b in range(stop, B + 1):
                body(b)

        block = ctx.enter_context(nc.Block())

        @block.tensor
        def _(pe):
            pe.wait_ge(consts_ready, 1)
            pe.wait_ge(mask_loaded, 16)
            for c in range(CH):
                mm = pe.transpose(st_ps[0][:, c * B:(c + 1) * B], mask_in[:, c * P:(c + 1) * P], ident[0:B, 0:B])
            mm.then_inc(mask_turned, 1)
            pe.wait_ge(silu_ready, 1)
            for k in range(KE):
                mm = pe.transpose(st_ps[1][:, k * B:(k + 1) * B], cond_silu[:, k * P:(k + 1) * P], ident[0:B, 0:B])
            mm.then_inc(cond_turned, 1)

            def embedding():
                pe.wait_ge(cond_ready, 1)
                pe.wait_ge(emb_loaded, EMB_DMAS * 16)
                for m in range(2 * KD):
                    for k in range(KE):
                        mm = pe.matmul(st_ps[0][:, m * B:(m + 1) * B], w_e[:, k, m * P:(m + 1) * P], cond_t[:, k, :],
                                       start=(k == 0), stop=(k == KE - 1))
                mm.then_inc(emb_ready, 1)

            def max_unit(b, t, h):
                ahead = t + MAX_LEAD
                mb, step = (b, ahead) if ahead < STEPS else (b + 1, ahead - STEPS)
                if not exists(mb):
                    return
                g, c = step // CH, step % CH
                if c == 0 and h == 0:
                    pe.wait_ge(rows_filled[g], ROW_DMAS * 16 * (mb + 1))
                u = GH * step + h
                wait(pe, max_done, UNITS * mb + bank_before(u, MX_BANKS) + 1)
                pe.matmul(mx_ps[bank_of(u, MX_BANKS)][:, :], q_rows[0:ROWS_MASK, g, h, c * P:(c + 1) * P],
                          k_rows[0:ROWS_MASK, g, h, :], start=True, stop=True).then_inc(max_ready, 1)

            def st_unit(b, t, h):
                if not exists(b):
                    return
                g, c = t // CH, t % CH
                if c == 0 and h == 0:
                    pe.wait_ge(max_filled[g], 2 * 16 * (b + 1))
                    if isinstance(b, int) and b == 0 and g == 0:
                        pe.wait_ge(setup_done, 1)
                u = GH * t + h
                wait(pe, exp_done, UNITS * b + bank_before(u, ST_BANKS) + 1)
                pe.matmul(st_ps[bank_of(u, ST_BANKS)][:, :], k_rows[0:ROWS_ALL, g, h, c * P:(c + 1) * P],
                          q_rows[0:ROWS_ALL, g, h, :], start=True, stop=True).then_inc(st_ready, 1)

            def pv_step(b, t):
                b, t = (b, t - 1) if t else (b - 1, STEPS - 1)
                if not exists(b):
                    return
                g, c = t // CH, t % CH
                if c == 0:
                    pe.wait_ge(v_ready, NG * b + g + 1)
                    wait(pe, yt_ready, NG * b + g)
                pe.wait_ge(exp_done, UNITS * b + GH * (t + 1))
                for h in range(GH):
                    mm = pe.matmul(pv_ps[VW * h:VW * (h + 1), :], v_rows[:, c, g * GH + h, :], probs[:, t % P_SLOTS, h, :],
                                   start=(c == 0), stop=(c == CH - 1), tile_position=(0, VW * h), skip_group_check=True)
                mm.then_inc(pv_done, 1)

            def job(at, b):
                _, _, kind, i, db = JOBS[at]
                if not job_exists(kind, i, db, b):
                    return
                ps, d = job_ps[at % JOB_BANKS], b + db
                freed = bank_freed(at, b)
                if freed:
                    wait(pe, *freed)
                if kind == "proj":
                    if isinstance(d, int) and d == 0 and i == 0:
                        pe.wait_ge(weights_loaded, WEIGHT_DMAS * 16)
                    pe.wait_ge(xt_ready, KD * (d + 1))
                    for k in range(KD):
                        mm = pe.matmul(ps[:, :], w_qk[:, k, i, :], x_norm_t[:, k, :], start=(k == 0), stop=(k == KD - 1))
                elif kind == "vproj":
                    pe.wait_ge(xt_ready, KD * (d + 1))
                    for c in range(2):
                        tok = (2 * i + c) * P
                        for k in range(KD):
                            mm = pe.matmul(ps[:, c * D:(c + 1) * D], x_norm_t[:, k, tok:tok + P], w_v[:, k, :],
                                           start=(k == 0), stop=(k == KD - 1))
                elif kind == "xturn":
                    pe.wait_ge(x_norm_ready, CH * (d + 1))
                    for c in range(CH):
                        mm = pe.transpose(ps[:, c * P:(c + 1) * P], x_norm[:, c, i * P:(i + 1) * P], ident[:, :])
                elif kind == "cturn":
                    pe.wait_ge(max_done, GH * CH * (NG * d + i + 1))
                    mm = pe.transpose(ps[0:GH * CH, 0:P], negmax[:, i % 2, :], ident[:, :])
                elif kind == "yturn":
                    pe.wait_ge(yt_ready, NG * d + i + 1)
                    for c in range(CH):
                        mm = pe.transpose(ps[:, c * P:(c + 1) * P], y_t[:, c * P:(c + 1) * P], ident[:, :])
                elif kind == "hturn":
                    pe.wait_ge(y_norm_ready, CH * (d + 1))
                    for c in range(CH):
                        mm = pe.transpose(ps[:, c * P:(c + 1) * P], y_norm[:, c, i * P:(i + 1) * P], ident[:, :])
                else:
                    pe.wait_ge(h_ready, KD * (d + 1))
                    for c in range(2):
                        tok = (2 * i + c) * P
                        for k in range(KD):
                            mm = pe.matmul(ps[:, c * D:(c + 1) * D], h_t[:, k, tok:tok + P], w_o[:, k, :],
                                           start=(k == 0), stop=(k == KD - 1))
                mm.then_inc(turned[kind], 1)

            def body(b):
                for t in range(STEPS):
                    for h in range(GH):
                        if h == GH // 2:
                            pv_step(b, t)
                            for n in jobs_at(t, MID):
                                job(n, b)
                        max_unit(b, t, h)
                        st_unit(b, t, h)
                    for n in jobs_at(t, END):
                        job(n, b)
                    if t == 5 and isinstance(b, int) and b == -1:
                        embedding()

            run(pe, body)

        @block.scalar
        def _(act):
            act.wait_ge(cond_loaded, 16)
            act.activation(cond_tanh[:, :], cond_in[:, :], ACT.Tanh, scale=0.5).then_inc(tanh_ready, 1)
            act.wait_ge(norm_loaded, 2 * 16)

            def exp_unit(b, t, h):
                if not exists(b):
                    return
                u = GH * t + h
                if h == 0:
                    wait(act, pv_done, STEPS * b + t - P_SLOTS + 1)
                act.wait_ge(st_ready, UNITS * b + u + 1)
                act.activation(probs[:, t % P_SLOTS, h, :], st_ps[bank_of(u, ST_BANKS)][:, :], ACT.Exp).then_inc(exp_done, 1)

            def read_job(at, b, half):
                _, _, kind, i, db = JOBS[at]
                if not job_exists(kind, i, db, b):
                    return
                ps, d = job_ps[at % JOB_BANKS], b + db
                if kind == "proj" and half == 1:
                    wait(act, parts_saved[0], 16 * (NG * d + i))
                    act.activation(qk_parts[:, 0, :], ps[:, :], ACT.Identity,
                                   bias=qkb_col[:, i:i + 1]).then_inc(part0_ready, 1)
                elif kind == "hturn" and half == 1:
                    act.activation(h_lin[:, i, :], ps[:, :], ACT.Identity, bias=mod_now[:, 1, i:i + 1],
                                   scale=mod_now[:, 0, i:i + 1]).then_inc(h_lin_ready, 1)
                elif half == 1:
                    return
                elif kind == "proj":
                    act.wait_ge(turned["proj"], NG * d + i + 1)
                    wait(act, rest_ready, NG * d + i)
                    act.activation(qk_full[:, :], ps[:, :], ACT.Identity, bias=qkb_col[:, i:i + 1])
                elif kind == "xturn":
                    act.wait_ge(turned["xturn"], KD * d + i + 1)
                    wait(act, turned["proj"], NG * d)
                    act.activation(x_norm_t[:, i, :], ps[:, :], ACT.Identity, bias=nb_col[:, i:i + 1],
                                   scale=nw_col[:, i:i + 1]).then_inc(xt_ready, 1)
                elif kind == "vproj":
                    act.wait_ge(turned["vproj"], 2 * d + i + 1)
                    wait(act, v_biased_ready, NG * d)
                    act.copy(v_plain[:, 2 * i:2 * i + 2, :], ps[:, :].rearrange("p (c f) -> p c f", f=D)
                             ).then_inc(v_plain_ready, 1)
                elif kind == "hturn":
                    act.wait_ge(turned["hturn"], KD * d + i + 1)
                    act.wait_ge(mod_ready, d + 1)
                    wait(act, h_ready, KD * d)
                    act.activation(h_tanh[:, i, :], ps[:, :], ACT.Tanh, bias=mod_now[:, 1, i:i + 1],
                                   scale=mod_now[:, 0, i:i + 1])
                elif kind == "cturn":
                    g = i % NG
                    act.wait_ge(max_split, NG * d + i + 1)
                    for part in range(2):
                        act.dma_start(
                            q_rows[ROWS_MASK + part:ROWS_MASK + part + 1, g, :, :].rearrange(
                                "p h (c t) -> p (h c) t", t=P),
                            max_parts[:, i % 2, part:part + 1, :]).then_inc(max_filled[g], 16)

            def yt_copy(b, t):
                n = t // CH - 1
                b, g = (b, n) if n >= 0 else (b - 1, NG - 1)
                if not exists(b):
                    return
                act.wait_ge(pv_done, STEPS * b + CH * (g + 1))
                wait(act, turned["yturn"], NG * b + g)
                act.copy(y_t[:, :], pv_ps[:, :]).then_inc(yt_ready, 1)

            def body(b):
                for t in range(STEPS):
                    exp_unit(b, t, 0)
                    exp_unit(b, t, 1)
                    for n in jobs_at(t - 1, END):
                        read_job(n, b, 1)
                    if t % CH == 0:
                        yt_copy(b, t)
                    for n in jobs_at(t, MID):
                        if JOBS[n][2] != "cturn":
                            read_job(n, b, 0)
                    exp_unit(b, t, 2)
                    exp_unit(b, t, 3)
                    for n in jobs_at(t, MID):
                        read_job(n, b, 0 if JOBS[n][2] == "cturn" else 1)
                    for n in jobs_at(t, END):
                        read_job(n, b, 0)

            run(act, body)

        @block.vector
        def _(dve):
            def mask_rows():
                dve.wait_ge(mask_loaded, 16)
                dve.tensor_scalar(mask_bias[:, :], mask_in[:, :], -1.0, MASKED, ALU.add, ALU.mult).then_inc(setup_chain, 1)
                dve.wait_ge(setup_chain, 2)
                dve.tensor_copy(mask_parts[:, 0, :], mask_bias[:, :]).then_inc(setup_chain, 1)
                dve.wait_ge(setup_chain, 3)
                dve.tensor_tensor(mask_rest[:, 0, :], mask_bias[:, :], mask_parts[:, 0, :], ALU.subtract).then_inc(setup_chain, 1)
                dve.wait_ge(setup_chain, 4)
                dve.tensor_copy(mask_parts[:, 1, :], mask_rest[:, 0, :]).then_inc(setup_chain, 1)
                dve.wait_ge(setup_chain, 5)
                dve.tensor_tensor(mask_rest[:, 1, :], mask_rest[:, 0, :], mask_parts[:, 1, :], ALU.subtract).then_inc(setup_chain, 1)
                dve.wait_ge(setup_chain, 6)
                dve.tensor_copy(mask_parts[:, 2, :], mask_rest[:, 1, :]).then_inc(maskp_ready, 1)
                dve.memset(k_rows[ROWS_PROD:P, :, :, :].bitcast(F32), TWO_ONES).then_inc(k_preset, 1)

            def silu_of_cond():
                dve.wait_ge(tanh_ready, 1)
                dve.scalar_tensor_tensor(cond_tanh[:, :], cond_tanh[:, :], 1.0, cond_in[:, :], ALU.add, ALU.mult
                                         ).then_inc(setup_chain, 1)
                dve.wait_ge(setup_chain, 1)
                dve.tensor_scalar(cond_silu[:, :], cond_tanh[:, :], 0.5, None, ALU.mult).then_inc(silu_ready, 1)
                dve.wait_ge(mask_turned, 1)
                dve.tensor_copy(mask_col[:, :, :], st_ps[0][:, 0:CH * B].rearrange("p (c b) -> p c b", b=B)
                                ).then_inc(mask_col_ready, 1)
                dve.wait_ge(cond_turned, 1)
                dve.tensor_copy(cond_t[:, :, :], st_ps[1][:, 0:KE * B].rearrange("p (k b) -> p k b", b=B)).then_inc(cond_ready, 1)

            def embedding():
                dve.wait_ge(emb_ready, 1)
                for m in range(2 * KD):
                    dve.tensor_scalar(emb_t[:, m, :], st_ps[0][:, m * B:(m + 1) * B], eb_col[:, m:m + 1],
                                      1.0 if m < KD else 0.0, ALU.add, ALU.add).then_inc(setup_chain, 1)
                dve.wait_ge(setup_chain, 6 + 2 * KD)
                for k in range(KD):
                    dve.tensor_scalar(mod_full[:, 0, k, :], emb_t[:, k, :], sbw_col[:, k:k + 1], None, ALU.mult)
                    dve.scalar_tensor_tensor(mod_full[:, 1, k, :], emb_t[:, k, :], sbb_col[:, k:k + 1], emb_t[:, KD + k, :],
                                             ALU.mult, ALU.add).then_inc(setup_chain, 1)
                dve.wait_ge(setup_chain, 6 + 3 * KD)
                dve.tensor_scalar(mod_half[:, :, :, :], mod_full[:, :, :, :], 0.5, None, ALU.mult).then_inc(setup_done, 1)

            def max_unit(b, t, h):
                ahead = t + MAX_LEAD
                mb, step = (b, ahead) if ahead < STEPS else (b + 1, ahead - STEPS)
                if not exists(mb):
                    return
                g, c = step // CH, step % CH
                if c == 0 and h == 0:
                    wait(dve, turned["cturn"], NG * mb + g - 1)
                dve.wait_ge(max_ready, UNITS * mb + GH * step + h + 1)
                dve.tensor_reduce(negmax[:, g % 2, h * CH + c:h * CH + c + 1], mx_ps[bank_of(GH * step + h, MX_BANKS)][:, :],
                                  AXIS_X, ALU.max, negate=True).then_inc(max_done, 1)

            def stats(src, raw, c):
                dve.bn_stats(raw[:, c, :], src[:, c, :]).then_inc(bn_ready, 1)

            def moments(raw, mv, negmean, vareps, ready, nth):
                dve.wait_ge(bn_ready, 2 * CH * nth + CH)
                dve.memset(spacer[:, :], 0.0)
                for c in range(CH):
                    dve.bn_aggr(mv[:, c, :], raw[:, c, :]).then_inc(bn_ready, 1)
                dve.wait_ge(bn_ready, 2 * CH * (nth + 1))
                dve.tensor_scalar(negmean[:, :], mv[:, :, 0], -1.0, None, ALU.mult)
                dve.tensor_scalar(vareps[:, :], mv[:, :, 1], EPS, None, ALU.add).then_inc(ready, 1)

            def split_max(at, b):
                _, _, kind, i, db = JOBS[at]
                if not job_exists(kind, i, db, b):
                    return
                ps, n = job_ps[at % JOB_BANKS], NG * b + i
                dve.wait_ge(turned["cturn"], n + 1)
                if not isinstance(b, int) or n >= 2:
                    lap, slot = (b, i - 2) if i >= 2 else (b - 1, i - 2 + NG)
                    dve.wait_ge(max_filled[slot], 2 * 16 * (lap + 1))
                dve.tensor_copy(max_parts[:, i % 2, 0, :], ps[0:GH * CH, 0:P]).then_inc(split_chain, 1)
                dve.wait_ge(split_chain, n + 1)
                dve.tensor_tensor(max_parts[:, i % 2, 1, :], ps[0:GH * CH, 0:P], max_parts[:, i % 2, 0, :],
                                  ALU.subtract).then_inc(max_split, 1)

            def read_job(at, b):
                _, _, kind, i, db = JOBS[at]
                if not job_exists(kind, i, db, b):
                    return
                ps, d = job_ps[at % JOB_BANKS], b + db
                if kind == "yturn":
                    by_head = ps[:, :].rearrange("p (c h w) -> p c h w", h=GH, w=VW)
                    dve.wait_ge(turned["yturn"], NG * d + i + 1)
                    wait(dve, y_ready, NG * d + i)
                    dve.reciprocal(y_recip[:, :, :], by_head[:, :, :, HD]).then_inc(recip_ready, 1)
                    dve.wait_ge(recip_ready, NG * d + i + 1)
                    wait(dve, y_norm_ready, CH * d)
                    dve.tensor_tensor(y[:, :, i * GC:(i + 1) * GC].rearrange("p c (h l) -> p c h l", l=HD),
                                      by_head[:, :, :, 0:HD],
                                      y_recip[:, :, :].unsqueeze(3).broadcast_to((P, CH, GH, HD)),
                                      ALU.mult).then_inc(y_ready, 1)
                elif kind == "outp":
                    dve.wait_ge(turned["outp"], 2 * d + i + 1)
                    dve.wait_ge(res_ready, d + 1)
                    wait(dve, out_saved, 2 * 16 * d)
                    dve.tensor_tensor(out_sb[:, 2 * i:2 * i + 2, :], ps[:, :].rearrange("p (c f) -> p c f", f=D),
                                      x_res[:, 2 * i:2 * i + 2, :], ALU.add).then_inc(out_ready, 1)

            def late_job(at, b):
                _, _, kind, i, db = JOBS[at]
                if not job_exists(kind, i, db, b):
                    return
                d = b + db
                if kind == "proj":
                    n = NG * d + i
                    dve.wait_ge(rest_ready, n + 1)
                    wait(dve, parts_saved[1], 16 * n)
                    dve.tensor_copy(qk_parts[:, 1, :], qk_rest[:, :]).then_inc(part1_ready, 1)
                elif kind == "hturn":
                    dve.wait_ge(h_lin_ready, KD * d + i + 1)
                    wait(dve, turned["outp"], 2 * d)
                    dve.scalar_tensor_tensor(h_t[:, i, :], h_tanh[:, i, :], 1.0, h_lin[:, i, :], ALU.add, ALU.mult
                                             ).then_inc(h_ready, 1)

            def x_stat(b, t, h):
                if not exists(b + 1):
                    return
                if t == 0:
                    if h == 0:
                        dve.wait_ge(x_loaded, X_DMAS * 16 * (b + 2))
                        wait(dve, x_norm_ready, CH * (b + 1))
                    stats(x_in, x_stats, h)
                elif h == 0:
                    moments(x_stats, x_mv, x_negmean, x_vareps, x_stat_ready, nth_stats(b, 0))

            def y_stat(b, t, h):
                if not exists(b - 1):
                    return
                if t == 3:
                    if h == 0:
                        dve.wait_ge(y_ready, NG * b)
                        wait(dve, y_norm_ready, CH * (b - 1))
                    stats(y, y_stats, h)
                elif h == 0:
                    moments(y_stats, y_mv, y_negmean, y_vareps, y_stat_ready, nth_stats(b, 1))

            def body(b):
                for t in range(STEPS):
                    for h in range(GH):
                        max_unit(b, t, h)
                        if h == 0:
                            for n in jobs_at(t - 1, END):
                                read_job(n, b)
                            for n in jobs_at(t - 2, END):
                                late_job(n, b)
                        if h == 1:
                            for n in jobs_at(t, MID):
                                if JOBS[n][2] == "cturn":
                                    split_max(n, b)
                            for n in jobs_at(t - 1, MID):
                                late_job(n, b)
                        if h == 2:
                            for n in jobs_at(t, MID):
                                read_job(n, b)
                        if t in (0, 1):
                            x_stat(b, t, h)
                        if t in (3, 4):
                            y_stat(b, t, h)
                    if t == 1 and isinstance(b, int) and b == -1:
                        silu_of_cond()
                        mask_rows()
                    if t == 7 and isinstance(b, int) and b == -1:
                        embedding()

            def nth_stats(b, which):
                if not isinstance(b, int):
                    return 2 * b + which
                return sum(exists(i + 1) + exists(i - 1) for i in range(-1, b)) + (which if exists(b + 1) else 0)

            run(dve, body)

        @block.gpsimd
        def _(pool):
            pool.memset(ident[:, :], 1.0).then_inc(pool_chain, 1)
            pool.memset(exponent[:, :], -0.5)
            pool.wait_ge(pool_chain, 1)
            pool.affine_select(ident[:, :], ident[:, :], pattern=[[-1, P]], compare_op=ALU.is_equal, fill=0.0,
                               base=0, channel_multiplier=1).then_inc(consts_ready, 1)
            pool.wait_ge(consts_ready, 1)
            def presets():
                pool.wait_ge(x_norm_ready, CH)
                pool.memset(q_rows[ROWS_PROD:P, :, :, :].bitcast(F32), TWO_ONES).then_inc(q_preset, 1)
                pool.wait_ge(q_preset, 1)
                pool.memset(v_rows[:, :, :, :], 0.0).then_inc(pool_chain, 1)
                pool.wait_ge(pool_chain, 2)
                pool.memset(v_rows[:, :, :, HD:HD + 1], 1.0).then_inc(pool_chain, 1)
                pool.wait_ge(pool_chain, 3)

            def norm(src, dst, negmean, vareps, rstd, stat_ready, rstd_ready, norm_ready, d):
                pool.wait_ge(stat_ready, d + 1)
                pool.tensor_tensor(rstd[:, :], vareps[:, :], exponent[:, :], ALU.pow).then_inc(rstd_ready, 1)
                wait_apart(pool, consts_ready, rstd_ready, d + 1)
                for c in range(CH):
                    pool.tensor_scalar(dst[:, c, :], src[:, c, :], negmean[:, c:c + 1], rstd[:, c:c + 1],
                                       ALU.add, ALU.mult).then_inc(norm_ready, 1)

            def take_rest(b, i, db):
                if not exists(b + db):
                    return
                n = NG * (b + db) + i
                pool.wait_ge(part0_ready, n + 1)
                wait(pool, part1_ready, n)
                wait(pool, part2_ready, n)
                pool.tensor_tensor(qk_rest[:, :], qk_full[:, :], qk_parts[:, 0, :], ALU.subtract).then_inc(rest_ready, 1)

            def take_part2(b, i, db):
                if not exists(b + db):
                    return
                n = NG * (b + db) + i
                pool.wait_ge(part1_ready, n + 1)
                wait(pool, parts_saved[2], 16 * n)
                pool.tensor_tensor(qk_parts[:, 2, :], qk_rest[:, :], qk_parts[:, 1, :], ALU.subtract).then_inc(part2_ready, 1)

            def values(b, g):
                if not exists(b):
                    return
                n = NG * b + g
                pool.wait_ge(v_plain_ready, 2 * (b + 1))
                wait(pool, v_ready, n)
                pool.tensor_tensor(v_biased[:, :, :], v_plain[:, :, g * GC:(g + 1) * GC],
                                   vb_row[:, g * GC:(g + 1) * GC].unsqueeze(1).broadcast_to((P, CH, GC)),
                                   ALU.add).then_inc(v_biased_ready, 1)
                pool.wait_ge(v_biased_ready, n + 1)
                wait(pool, pv_done, STEPS * (b - 1) + CH * (g + 1))
                pool.tensor_tensor(v_rows[:, :, g * GH:(g + 1) * GH, 0:HD],
                                   v_biased[:, :, :].rearrange("p c (h l) -> p c h l", l=HD),
                                   mask_now[:, :].unsqueeze(2).unsqueeze(3).broadcast_to((P, CH, GH, HD)),
                                   ALU.mult).then_inc(v_ready, 1)

            def body(b):
                take_rest(b, 3, 0)
                if exists(b + 1):
                    wait(pool, turned["xturn"], KD * (b + 1))
                    norm(x_in, x_norm, x_negmean, x_vareps, x_rstd, x_stat_ready, x_rstd_ready, x_norm_ready, b + 1)
                take_part2(b, 3, 0)
                if isinstance(b, int) and b == -1:
                    presets()
                values(b, 3)
                if exists(b - 1):
                    wait(pool, turned["hturn"], KD * (b - 1))
                    norm(y, y_norm, y_negmean, y_vareps, y_rstd, y_stat_ready, y_rstd_ready, y_norm_ready, b - 1)
                    wait(pool, h_lin_ready, KD * (b - 1))
                    if isinstance(b, int) and b == 1:
                        pool.wait_ge(setup_done, 1)
                    pool.tensor_copy(mod_now[:, :, :], mod_half[:, :, :, bass.ds(b - 1, 1)].rearrange("p a k b -> p a (k b)")
                                     ).then_inc(mod_ready, 1)
                for g in range(NG - 1):
                    take_rest(b, g, 1)
                    take_part2(b, g, 1)
                    if g == 0 and exists(b + 1):
                        wait(pool, v_ready, NG * (b + 1))
                        if isinstance(b, int) and b == -1:
                            pool.wait_ge(mask_col_ready, 1)
                        pool.tensor_copy(mask_now[:, :], mask_col[:, :, bass.ds(b + 1, 1)].rearrange("p c b -> p (c b)")
                                         ).then_inc(now_ready, 1)
                        pool.wait_ge(now_ready, b + 2)
                    values(b + 1, g)
                    if g == 0 and exists(b - 1):
                        pool.wait_ge(res_loaded, 16 * b)
                        pool.tensor_tensor(x_res[:, :, :], x_res[:, :, :],
                                           ob_row[:, :].unsqueeze(1).broadcast_to((P, CH, D)), ALU.add).then_inc(res_ready, 1)

            run(pool, body)

        @block.sync
        def _(sp):
            for c in range(X_DMAS):
                sp.dma_start(x_in[:, 2 * c:2 * c + 2, :], batch_of(x_dram, 0)[:, 2 * c:2 * c + 2, :]).then_inc(x_loaded, 16)
            with nc.allow_non_contiguous_dma(reason="small vectors, once"):
                for dst, src in ((nb_col, norm_b), (nw_col, norm_w)):
                    sp.dma_start(dst[:, :], src.rearrange("(k p) -> p k", p=P)).then_inc(norm_loaded, 16)
                sp.dma_start(cond_in[:, :], cond[:, :]).then_inc(cond_loaded, 16)
                sp.dma_start(mask_in[:, :], mask[:, :]).then_inc(mask_loaded, 16)
                loads = [(w_qk[:, k, :, n * GC:(n + 1) * GC], w[k * P:(k + 1) * P, :].rearrange("p (g c) -> p g c", c=GC))
                         for k in range(KD) for n, w in enumerate((q_w, k_w))]
                for n, src in enumerate((q_b, k_b)):
                    loads.append((qkb_col[n * GC:(n + 1) * GC, :], src.rearrange("(g c) -> c g", c=GC)))
                loads.append((w_v[:, :, :], v_w.rearrange("(k p) n -> p k n", p=P)))
                loads.append((vb_row[:, :], v_b.rearrange("(a n) -> a n", a=1).broadcast_to((P, D))))
                assert len(loads) == WEIGHT_DMAS
                for dst, src in loads:
                    sp.dma_start(dst, src).then_inc(weights_loaded, 16)
                loads = [(sbw_col[:, :], sb_w.rearrange("(k p) -> p k", p=P)),
                         (sbb_col[:, :], sb_b.rearrange("(k p) -> p k", p=P)),
                         (eb_col[:, :], emb_b.rearrange("(k p) -> p k", p=P)),
                         (ob_row[:, :], out_b.rearrange("(a n) -> a n", a=1).broadcast_to((P, D))),
                         (w_e[:, :, :], emb_w.rearrange("(k p) n -> p k n", p=P)),
                         (w_o[:, :, :], out_w.rearrange("(k p) n -> p k n", p=P))]
                assert len(loads) == EMB_DMAS
                for dst, src in loads:
                    sp.dma_start(dst, src).then_inc(emb_loaded, 16)
            sp.wait_ge(maskp_ready, 1)
            sp.dma_start(mask_dram[:, :, :], mask_parts[:, :, :]).then_inc(mask_saved, 16)
            sp.wait_ge(mask_saved, 16)
            sp.wait_ge(q_preset, 1)
            sp.wait_ge(k_preset, 1)

            def spread(b, i, db):
                d = b + db
                if not exists(d):
                    return
                n = NG * d + i
                for part, ready in enumerate((part0_ready, part1_ready, part2_ready)):
                    sp.wait_ge(ready, n + 1)
                    sp.dma_start(qk_dram[i, part].rearrange("l h t -> h l t"), qk_parts[:, part, :]
                                 ).then_inc(parts_saved[part], 16)
                sp.dma_start(k_rows[ROWS_PROD:ROWS_MASK, i, :, :],
                             mask_dram[bass.ds(d, 1)].rearrange("a s t -> (a s) t").unsqueeze(1).broadcast_to(
                                 (PARTS, GH, T))).then_inc(rows_filled[i], 16)
                q_src, k_src = (qk_dram[i, :, :, m * GH:(m + 1) * GH, :].rearrange("s l h t -> s l (h t)") for m in range(2))
                for part in range(PARTS):
                    sp.wait_ge(parts_saved[part], 16 * (n + 1))
                    first, count = (0, 3, 5)[part], PARTS - part
                    sp.dma_start(k_rows[first * HD:(first + count) * HD, i, :, :].rearrange("p h t -> p (h t)"),
                                 k_src[part:part + 1].broadcast_to((count, HD, GH * T))).then_inc(rows_filled[i], 16)
                for first, count in ((0, 3), (3, 2), (5, 1)):
                    sp.dma_start(q_rows[first * HD:(first + count) * HD, i, :, :].rearrange("p h t -> p (h t)"),
                                 q_src[0:count]).then_inc(rows_filled[i], 16)

            def store(b, i):
                if not exists(b):
                    return
                wait_apart(sp, maskp_ready, out_ready, 2 * b + i + 1)
                sp.dma_start(batch_of(out_dram, b)[:, 2 * i:2 * i + 2, :], out_sb[:, 2 * i:2 * i + 2, :]
                             ).then_inc(out_saved, 16)

            def body(b):
                if exists(b - 1):
                    wait_apart(sp, maskp_ready, out_ready, 2 * (b - 1))
                    sp.dma_start(x_res[:, :, :], batch_of(x_dram, b - 1)).then_inc(res_loaded, 16)
                spread(b, 3, 0)
                if exists(b + 2):
                    wait_apart(sp, maskp_ready, x_norm_ready, CH * (b + 2))
                    for c in range(X_DMAS):
                        sp.dma_start(x_in[:, 2 * c:2 * c + 2, :], batch_of(x_dram, b + 2)[:, 2 * c:2 * c + 2, :]
                                     ).then_inc(x_loaded, 16)
                spread(b, 0, 1)
                spread(b, 1, 1)
                for i in range(2):
                    if exists(b - 1):
                        wait_apart(sp, maskp_ready, out_ready, 2 * (b - 1) + i + 1)
                        sp.dma_start(batch_of(out_dram, b - 1)[:, 2 * i:2 * i + 2, :], out_sb[:, 2 * i:2 * i + 2, :]
                                     ).then_inc(out_saved, 16)
                    if i == 0:
                        spread(b, 2, 1)

            run(sp, body, B - 2)
            sp.wait_ge(out_saved, 2 * 16 * B)


X_DMAS = 2
WEIGHT_DMAS = 2 * KD + 2 + 2
EMB_DMAS = 6
ROW_DMAS = 7

_INS = ["x", "cond_2048", "mask_BxS_ff1", "L0_cond_norm_w", "L0_cond_norm_b", "L0_cond_q_w", "L0_cond_q_b",
        "L0_cond_k_w", "L0_cond_k_b", "L0_cond_v_w", "L0_cond_v_b", "L0_cond_emb_w", "L0_cond_emb_b",
        "L0_cond_sb_norm_w", "L0_cond_sb_norm_b", "L0_cond_out_w", "L0_cond_out_b"]


def kernel(**inputs):
    import numpy as _np
    import concourse.bacc as _bacc
    from concourse import mybir as _mybir
    from concourse.bass_utils import run_bass_kernel_spmd as _run

    nc = _bacc.Bacc("TRN2", target_bir_lowering=False, num_devices=1)
    arrays, args = {}, []
    for name in _INS:
        a = _np.ascontiguousarray(inputs[name])
        arrays[f"in_{name}"] = a
        args.append(nc.dram_tensor(f"in_{name}", a.shape, _mybir.dt.from_np(a.dtype), kind="ExternalInput").ap())
    args.append(nc.dram_tensor("out_0", (B, T, D), F32, kind="ExternalOutput").ap())
    attention_layer(nc, *args)
    r = _run(nc, [arrays], core_ids=[0])
    return r.results[0]["out_0"]
```

```python
from contextlib import ExitStack

import concourse.bass as bass
from concourse import mybir

F32 = mybir.dt.float32
BF16 = mybir.dt.bfloat16
ALU = mybir.AluOpType
ACT = mybir.ActivationFunctionType
AXIS_X = mybir.AxisListType.X

P = 128
B, T, D = 8, 512, 256
HEADS = 16
HD = D // HEADS
TE = 512
EPS = 1e-5
MASKED = 1000000.0
CH = T // P
KD = D // P
KE = TE // P
GH = 4
NG = HEADS // GH
GC = GH * HD
STEPS = NG * CH
UNITS = STEPS * GH
MAX_LEAD = 6
P_SLOTS = 4
ST_BANKS = 2
MX_BANKS = 3
JOB_BANKS = 2
PARTS = 3
ROWS_PROD = 6 * HD
ROWS_MASK = ROWS_PROD + PARTS
ROWS_ALL = ROWS_MASK + 2
VW = 32

X_DMAS = 2
WEIGHT_DMAS = 2 * KD + 2 + 2
EMB_DMAS = 6
ROW_DMAS = 7

TWO_ONES = 1.0 + 0x3F80 / 2 ** 23

MID, END = range(2)
JOBS = [
    (0, END, "yturn", 3, -1), (1, END, "proj", 3, 0), (2, MID, "cturn", 1, 0), (3, END, "xturn", 0, 1),
    (4, END, "xturn", 1, 1), (5, END, "proj", 0, 1), (6, MID, "cturn", 2, 0), (6, END, "hturn", 0, -1),
    (7, MID, "vproj", 0, 1), (7, END, "yturn", 0, 0), (8, END, "hturn", 1, -1), (9, END, "proj", 1, 1),
    (10, MID, "cturn", 3, 0), (10, END, "vproj", 1, 1), (11, END, "yturn", 1, 0), (12, END, "outp", 0, -1),
    (13, END, "proj", 2, 1), (14, MID, "cturn", 4, 0), (14, END, "outp", 1, -1), (15, END, "yturn", 2, 0),
]


EARLIER = {("proj", 1): 7, ("vproj", 1): 8, ("proj", 2): 9}


TURN_STEP = 4
EMBEDDING_STEP = 11
WARM_FIRST = {4: 4, 7: 6, 9: 2}
WARM_LAST = {0: 24, 8: 10}

X_STAT = [(0, 1), (0, 3), (1, 0), (1, 1), (1, 3)]
Y_STAT = [(3, 2), (3, 3), (4, 2), (4, 3), (5, 1)]


def jobs_at(b, step, place):
    if step < 0:
        b, step = b - 1, step + STEPS
    moved = EARLIER if isinstance(b, int) and b == -1 else {}
    return [(n, b) for n, j in enumerate(JOBS) if (moved.get(j[2:4], j[0]), j[1]) == (step, place)]


def bank_of(unit, banks):
    return unit % banks if unit < UNITS - 1 else 1


def bank_before(unit, banks):
    return next(v for v in range(unit - 1, unit - UNITS, -1) if bank_of(v % UNITS, banks) == bank_of(unit, banks))


def exists(batch):
    return not isinstance(batch, int) or 0 <= batch < B


def job_exists(kind, i, db, b):
    if kind == "cturn" and i == NG:
        return exists(b + 1)
    return exists(b + db)


def wait(engine, semaphore, count):
    if not isinstance(count, int) or count > 0:
        engine.wait_ge(semaphore, count)


def wait_apart(engine, met, semaphore, count):
    if not isinstance(count, int):
        engine.wait_ge(met, 1)
    wait(engine, semaphore, count)


def attention_layer(nc, x, cond, mask, norm_w, norm_b, q_w, q_b, k_w, k_b, v_w, v_b,
                    emb_w, emb_b, sb_w, sb_b, out_w, out_b, out):
    with ExitStack() as ctx:
        def sb(name, shape, dt=F32):
            return ctx.enter_context(nc.sbuf_tensor(name, shape, dt))

        def psum(name, shape, dt=F32):
            return ctx.enter_context(nc.psum_tensor(name, shape, dt))

        def sem(name):
            return ctx.enter_context(nc.semaphore(name))

        w_qk = sb("w_qk", [P, KD, NG, 2 * GC])
        w_v = sb("w_v", [P, KD, D])
        w_o = sb("w_o", [P, KD, D])
        w_e = sb("w_e", [P, KE, 2 * D])
        nw_col = sb("nw_col", [P, KD])
        nb_col = sb("nb_col", [P, KD])
        sbw_col = sb("sbw_col", [P, KD])
        sbb_col = sb("sbb_col", [P, KD])
        eb_col = sb("eb_col", [P, 2 * KD])
        qkb_col = sb("qkb_col", [P, NG])
        vb_row = sb("vb_row", [P, D])
        ob_row = sb("ob_row", [P, D])
        ident = sb("ident", [P, P])
        exponent = sb("exponent", [P, CH])
        cond_in = sb("cond_in", [B, TE])
        cond_tanh = sb("cond_tanh", [B, TE])
        cond_silu = sb("cond_silu", [B, TE])
        cond_t = sb("cond_t", [P, KE, B])
        emb_t = sb("emb_t", [P, 2 * KD, B])
        mod_full = sb("mod_full", [P, 2, KD, B])
        mod_half = sb("mod_half", [P, 2, KD, B])
        mod_now = sb("mod_now", [P, 2, KD])
        mask_in = sb("mask_in", [B, T])
        mask_bias = sb("mask_bias", [B, T])
        mask_rest = sb("mask_rest", [B, 2, T])
        mask_parts = sb("mask_parts", [B, PARTS, T], BF16)
        mask_col = sb("mask_col", [P, CH, B])
        mask_now = sb("mask_now", [P, CH])
        warm_in = sb("warm_in", [P, T], BF16)
        x_in = sb("x_in", [P, CH, D])
        spacer = sb("spacer", [P, 1])
        x_stats = sb("x_stats", [P, CH, 6])
        x_mv = sb("x_mv", [P, CH, 2])
        x_negmean = sb("x_negmean", [P, CH])
        x_vareps = sb("x_vareps", [P, CH])
        x_rstd = sb("x_rstd", [P, CH])
        x_norm = sb("x_norm", [P, CH, D])
        x_norm_t = sb("x_norm_t", [P, KD, T])
        qk_full = sb("qk_full", [P, T])
        qk_rest = sb("qk_rest", [P, T])
        qk_parts = sb("qk_parts", [P, PARTS, T], BF16)
        q_rows = sb("q_rows", [P, NG, GH, T], BF16)
        k_rows = sb("k_rows", [P, NG, GH, T], BF16)
        negmax = sb("negmax", [P, 2, GH * CH])
        max_parts = sb("max_parts", [GH * CH, 2, 2, P], BF16)
        v_plain = sb("v_plain", [P, CH, D])
        v_biased = sb("v_biased", [P, CH, GC])
        v_rows = sb("v_rows", [P, CH, HEADS, VW])
        probs = sb("probs", [P, P_SLOTS, GH, T])
        y_t = sb("y_t", [P, T])
        y_recip = sb("y_recip", [P, CH, GH])
        y = sb("y", [P, CH, D])
        y_stats = sb("y_stats", [P, CH, 6])
        y_mv = sb("y_mv", [P, CH, 2])
        y_negmean = sb("y_negmean", [P, CH])
        y_vareps = sb("y_vareps", [P, CH])
        y_rstd = sb("y_rstd", [P, CH])
        y_norm = sb("y_norm", [P, CH, D])
        h_tanh = sb("h_tanh", [P, KD, T])
        h_lin = sb("h_lin", [P, KD, T])
        h_t = sb("h_t", [P, KD, T])
        x_res = sb("x_res", [P, CH, D])
        out_sb = sb("out_sb", [P, CH, D])
        st_ps = [psum(f"st_ps{i}", [P, T]) for i in range(ST_BANKS)]
        mx_ps = [psum(f"mx_ps{i}", [P, T]) for i in range(MX_BANKS)]
        pv_ps = psum("pv_ps", [P, T])
        job_ps = [psum(f"job_ps{i}", [P, T]) for i in range(JOB_BANKS)]
        qk_dram = nc.dram_tensor("qk_dram", (NG, PARTS, HD, 2 * GH, T), BF16, kind="Internal").ap()
        mask_dram = nc.dram_tensor("mask_dram", (B, PARTS, T), BF16, kind="Internal").ap()

        x_loaded = sem("x_loaded")
        res_loaded = sem("res_loaded")
        cond_loaded = sem("cond_loaded")
        mask_loaded = sem("mask_loaded")
        norm_loaded = sem("norm_loaded")
        weights_loaded = sem("weights_loaded")
        mask_saved = sem("mask_saved")
        parts_saved = [sem(f"parts_saved{i}") for i in range(PARTS)]
        rows_filled = [sem(f"rows_filled{i}") for i in range(NG)]
        max_filled = [sem(f"max_filled{i}") for i in range(NG)]
        out_saved = sem("out_saved")
        warm_ready = sem("warm_ready")
        consts_ready = sem("consts_ready")
        q_preset = sem("q_preset")
        k_preset = sem("k_preset")
        tanh_ready = sem("tanh_ready")
        mask_turned = sem("mask_turned")
        mask_col_ready = sem("mask_col_ready")
        silu_ready = sem("silu_ready")
        cond_turned = sem("cond_turned")
        cond_ready = sem("cond_ready")
        emb_ready = sem("emb_ready")
        emb_loaded = sem("emb_loaded")
        maskp_ready = sem("maskp_ready")
        setup_chain = sem("setup_chain")
        pool_chain = sem("pool_chain")
        split_chain = sem("split_chain")
        setup_done = sem("setup_done")
        max_ready = sem("max_ready")
        st_ready = sem("st_ready")
        pv_done = sem("pv_done")
        turned = {k: sem(f"{k}_done") for k in ("proj", "yturn", "cturn", "xturn", "hturn", "outp", "vproj")}
        max_done = sem("max_done")
        exp_done = sem("exp_done")
        part0_ready = sem("part0_ready")
        rest_ready = sem("rest_ready")
        part1_ready = sem("part1_ready")
        part2_ready = sem("part2_ready")
        max_split = sem("max_split")
        xt_ready = sem("xt_ready")
        v_plain_ready = sem("v_plain_ready")
        v_biased_ready = sem("v_biased_ready")
        v_ready = sem("v_ready")
        yt_ready = sem("yt_ready")
        recip_ready = sem("recip_ready")
        y_ready = sem("y_ready")
        bn_ready = sem("bn_ready")
        x_stat_ready = sem("x_stat_ready")
        x_rstd_ready = sem("x_rstd_ready")
        x_norm_ready = sem("x_norm_ready")
        y_stat_ready = sem("y_stat_ready")
        y_rstd_ready = sem("y_rstd_ready")
        y_norm_ready = sem("y_norm_ready")
        now_ready = sem("now_ready")
        mod_ready = sem("mod_ready")
        h_lin_ready = sem("h_lin_ready")
        h_ready = sem("h_ready")
        res_ready = sem("res_ready")
        out_ready = sem("out_ready")

        x_dram = x.rearrange("b (c p) f -> b p c f", p=P)
        out_dram = out.rearrange("b (c p) f -> b p c f", p=P)

        def batch_of(view, batch):
            return view[bass.ds(batch, 1)].rearrange("a p c f -> (a p) c f")

        def emptied(kind, i, batch):
            if kind == "proj":
                return part0_ready, NG * batch + i + 1
            if kind == "yturn":
                return y_ready, NG * batch + i + 1
            if kind == "cturn":
                return max_split, NG * batch + i + 1
            of = {"xturn": xt_ready, "vproj": v_plain_ready, "hturn": h_lin_ready, "outp": out_ready}[kind]
            return of, 2 * batch + i + 1

        def bank_freed(at, b):
            for back in range(at - JOB_BANKS, at - 2 * len(JOBS), -JOB_BANKS):
                _, _, kind, i, db = JOBS[back % len(JOBS)]
                loop_b = b + back // len(JOBS)
                if isinstance(loop_b, int) and loop_b < -1:
                    return None
                if job_exists(kind, i, db, loop_b):
                    return emptied(kind, i, loop_b + db)
            return None

        def run(engine, body, stop=B - 1):
            for b in (-1, 0, 1):
                body(b)
            with engine.Fori(2, stop) as b:
                body(b)
            for b in range(stop, B + 1):
                body(b)

        block = ctx.enter_context(nc.Block())

        @block.tensor
        def _(pe):
            def keep_warm(ps, count):
                for _ in range(count):
                    pe.matmul(ps[:, :], warm_in[:, 0:P], warm_in[:, :], start=True, stop=True)

            pe.wait_ge(warm_ready, 1)
            keep_warm(pv_ps, 8)
            pe.wait_ge(consts_ready, 1)
            pe.wait_ge(mask_loaded, 16)
            for c in range(CH):
                mm = pe.transpose(st_ps[0][:, c * B:(c + 1) * B], mask_in[:, c * P:(c + 1) * P], ident[0:B, 0:B])
            mm.then_inc(mask_turned, 1)
            keep_warm(pv_ps, 7)

            def turn_cond():
                pe.wait_ge(silu_ready, 1)
                for k in range(KE):
                    mm = pe.transpose(st_ps[1][:, k * B:(k + 1) * B], cond_silu[:, k * P:(k + 1) * P], ident[0:B, 0:B])
                mm.then_inc(cond_turned, 1)

            def embedding(m):
                if m == 0:
                    pe.wait_ge(cond_ready, 1)
                    pe.wait_ge(emb_loaded, EMB_DMAS * 16)
                    pe.wait_ge(part0_ready, NG - 1)
                for k in range(KE):
                    mm = pe.matmul(job_ps[0][:, m * B:(m + 1) * B], w_e[:, k, m * P:(m + 1) * P], cond_t[:, k, :],
                                   start=(k == 0), stop=(k == KE - 1))
                mm.then_inc(emb_ready, 1)

            def max_unit(b, t, h):
                ahead = t + MAX_LEAD
                mb, step = (b, ahead) if ahead < STEPS else (b + 1, ahead - STEPS)
                if not exists(mb):
                    return
                g, c = step // CH, step % CH
                if c == 0 and h == 0:
                    pe.wait_ge(rows_filled[g], ROW_DMAS * 16 * (mb + 1))
                u = GH * step + h
                wait(pe, max_done, UNITS * mb + bank_before(u, MX_BANKS) + 1)
                pe.matmul(mx_ps[bank_of(u, MX_BANKS)][:, :], q_rows[0:ROWS_MASK, g, h, c * P:(c + 1) * P],
                          k_rows[0:ROWS_MASK, g, h, :], start=True, stop=True).then_inc(max_ready, 1)

            def st_unit(b, t, h):
                if not exists(b):
                    return
                g, c = t // CH, t % CH
                if c == 0 and h == 0:
                    pe.wait_ge(max_filled[g], 2 * 16 * (b + 1))
                    if isinstance(b, int) and b == 0 and g == 0:
                        pe.wait_ge(mask_col_ready, 1)
                        pe.wait_ge(cond_ready, 1)
                u = GH * t + h
                wait(pe, exp_done, UNITS * b + bank_before(u, ST_BANKS) + 1)
                pe.matmul(st_ps[bank_of(u, ST_BANKS)][:, :], k_rows[0:ROWS_ALL, g, h, c * P:(c + 1) * P],
                          q_rows[0:ROWS_ALL, g, h, :], start=True, stop=True).then_inc(st_ready, 1)

            def pv_step(b, t):
                b, t = (b, t - 1) if t else (b - 1, STEPS - 1)
                if not exists(b):
                    return
                g, c = t // CH, t % CH
                if c == 0:
                    pe.wait_ge(v_ready, NG * b + g + 1)
                    wait(pe, yt_ready, NG * b + g)
                pe.wait_ge(exp_done, UNITS * b + GH * (t + 1))
                for h in range(GH):
                    mm = pe.matmul(pv_ps[VW * h:VW * (h + 1), :], v_rows[:, c, g * GH + h, :], probs[:, t % P_SLOTS, h, :],
                                   start=(c == 0), stop=(c == CH - 1), tile_position=(0, VW * h), skip_group_check=True)
                mm.then_inc(pv_done, 1)

            def job(at, b):
                _, _, kind, i, db = JOBS[at]
                if not job_exists(kind, i, db, b):
                    return
                ps, d = job_ps[at % JOB_BANKS], b + db
                freed = bank_freed(at, b)
                if isinstance(b, int) and b == 0 and at == JOB_BANKS:
                    pe.wait_ge(setup_done, 1)
                if freed:
                    wait(pe, *freed)
                if kind == "proj":
                    if isinstance(d, int) and d == 0 and i == 0:
                        pe.wait_ge(weights_loaded, WEIGHT_DMAS * 16)
                    pe.wait_ge(xt_ready, KD * (d + 1))
                    for k in range(KD):
                        mm = pe.matmul(ps[:, :], w_qk[:, k, i, :], x_norm_t[:, k, :], start=(k == 0), stop=(k == KD - 1))
                elif kind == "vproj":
                    pe.wait_ge(xt_ready, KD * (d + 1))
                    for c in range(2):
                        tok = (2 * i + c) * P
                        for k in range(KD):
                            mm = pe.matmul(ps[:, c * D:(c + 1) * D], x_norm_t[:, k, tok:tok + P], w_v[:, k, :],
                                           start=(k == 0), stop=(k == KD - 1))
                elif kind == "xturn":
                    pe.wait_ge(x_norm_ready, CH * (d + 1))
                    for c in range(CH):
                        mm = pe.transpose(ps[:, c * P:(c + 1) * P], x_norm[:, c, i * P:(i + 1) * P], ident[:, :])
                elif kind == "cturn":
                    pe.wait_ge(max_done, GH * CH * (NG * d + i + 1))
                    mm = pe.transpose(ps[0:GH * CH, 0:P], negmax[:, i % 2, :], ident[:, :])
                elif kind == "yturn":
                    pe.wait_ge(yt_ready, NG * d + i + 1)
                    for c in range(CH):
                        mm = pe.transpose(ps[:, c * P:(c + 1) * P], y_t[:, c * P:(c + 1) * P], ident[:, :])
                elif kind == "hturn":
                    pe.wait_ge(y_norm_ready, CH * (d + 1))
                    for c in range(CH):
                        mm = pe.transpose(ps[:, c * P:(c + 1) * P], y_norm[:, c, i * P:(i + 1) * P], ident[:, :])
                else:
                    pe.wait_ge(h_ready, KD * (d + 1))
                    for c in range(2):
                        tok = (2 * i + c) * P
                        for k in range(KD):
                            mm = pe.matmul(ps[:, c * D:(c + 1) * D], h_t[:, k, tok:tok + P], w_o[:, k, :],
                                           start=(k == 0), stop=(k == KD - 1))
                mm.then_inc(turned[kind], 1)

            def body(b):
                for t in range(STEPS):
                    for h in range(GH):
                        if h == GH // 2:
                            pv_step(b, t)
                            for n, at_b in jobs_at(b, t, MID):
                                job(n, at_b)
                        max_unit(b, t, h)
                        st_unit(b, t, h)
                        if isinstance(b, int) and b == -1 and t + MAX_LEAD >= STEPS:
                            keep_warm(pv_ps, 1)
                    for n, at_b in jobs_at(b, t, END):
                        job(n, at_b)
                    if isinstance(b, int) and b == -1 and t == TURN_STEP:
                        turn_cond()
                    if isinstance(b, int) and b == -1 and 0 <= t - EMBEDDING_STEP < 2 * KD:
                        embedding(t - EMBEDDING_STEP)
                    if isinstance(b, int) and b == -1 and t in WARM_FIRST:
                        keep_warm(pv_ps, WARM_FIRST[t])
                    if isinstance(b, int) and b == B and t in WARM_LAST:
                        keep_warm(mx_ps[0], WARM_LAST[t])

            run(pe, body)

        @block.scalar
        def _(act):
            act.wait_ge(cond_loaded, 16)
            act.activation(cond_tanh[:, :], cond_in[:, :], ACT.Tanh, scale=0.5).then_inc(tanh_ready, 1)
            act.wait_ge(norm_loaded, 2 * 16)

            def exp_unit(b, t, h):
                if not exists(b):
                    return
                u = GH * t + h
                if h == 0:
                    wait(act, pv_done, STEPS * b + t - P_SLOTS + 1)
                act.wait_ge(st_ready, UNITS * b + u + 1)
                act.activation(probs[:, t % P_SLOTS, h, :], st_ps[bank_of(u, ST_BANKS)][:, :], ACT.Exp).then_inc(exp_done, 1)

            def read_job(at, b, half):
                _, _, kind, i, db = JOBS[at]
                if not job_exists(kind, i, db, b):
                    return
                ps, d = job_ps[at % JOB_BANKS], b + db
                if kind == "proj" and half == 1:
                    wait(act, parts_saved[0], 16 * (NG * d + i))
                    act.activation(qk_parts[:, 0, :], ps[:, :], ACT.Identity,
                                   bias=qkb_col[:, i:i + 1]).then_inc(part0_ready, 1)
                elif kind == "hturn" and half == 1:
                    act.activation(h_lin[:, i, :], ps[:, :], ACT.Identity, bias=mod_now[:, 1, i:i + 1],
                                   scale=mod_now[:, 0, i:i + 1]).then_inc(h_lin_ready, 1)
                elif half == 1:
                    return
                elif kind == "proj":
                    act.wait_ge(turned["proj"], NG * d + i + 1)
                    wait(act, rest_ready, NG * d + i)
                    act.activation(qk_full[:, :], ps[:, :], ACT.Identity, bias=qkb_col[:, i:i + 1])
                elif kind == "xturn":
                    act.wait_ge(turned["xturn"], KD * d + i + 1)
                    wait(act, turned["proj"], NG * d)
                    act.activation(x_norm_t[:, i, :], ps[:, :], ACT.Identity, bias=nb_col[:, i:i + 1],
                                   scale=nw_col[:, i:i + 1]).then_inc(xt_ready, 1)
                elif kind == "vproj":
                    act.wait_ge(turned["vproj"], 2 * d + i + 1)
                    wait(act, v_biased_ready, NG * d)
                    act.copy(v_plain[:, 2 * i:2 * i + 2, :], ps[:, :].rearrange("p (c f) -> p c f", f=D)
                             ).then_inc(v_plain_ready, 1)
                elif kind == "hturn":
                    act.wait_ge(turned["hturn"], KD * d + i + 1)
                    act.wait_ge(mod_ready, d + 1)
                    wait(act, h_ready, KD * d)
                    act.activation(h_tanh[:, i, :], ps[:, :], ACT.Tanh, bias=mod_now[:, 1, i:i + 1],
                                   scale=mod_now[:, 0, i:i + 1])
                elif kind == "cturn":
                    g = i % NG
                    act.wait_ge(max_split, NG * d + i + 1)
                    for part in range(2):
                        act.dma_start(
                            q_rows[ROWS_MASK + part:ROWS_MASK + part + 1, g, :, :].rearrange(
                                "p h (c t) -> p (h c) t", t=P),
                            max_parts[:, i % 2, part:part + 1, :]).then_inc(max_filled[g], 16)

            def yt_copy(b, t):
                n = t // CH - 1
                b, g = (b, n) if n >= 0 else (b - 1, NG - 1)
                if not exists(b):
                    return
                act.wait_ge(pv_done, STEPS * b + CH * (g + 1))
                wait(act, turned["yturn"], NG * b + g)
                act.copy(y_t[:, :], pv_ps[:, :]).then_inc(yt_ready, 1)

            def body(b):
                for t in range(STEPS):
                    exp_unit(b, t, 0)
                    exp_unit(b, t, 1)
                    for n, at_b in jobs_at(b, t - 1, END):
                        read_job(n, at_b, 1)
                    if t % CH == 0:
                        yt_copy(b, t)
                    for n, at_b in jobs_at(b, t, MID):
                        if JOBS[n][2] != "cturn":
                            read_job(n, at_b, 0)
                    exp_unit(b, t, 2)
                    exp_unit(b, t, 3)
                    for n, at_b in jobs_at(b, t, MID):
                        read_job(n, at_b, 0 if JOBS[n][2] == "cturn" else 1)
                    for n, at_b in jobs_at(b, t, END):
                        read_job(n, at_b, 0)

            run(act, body)

        @block.vector
        def _(dve):
            dve.memset(warm_in[:, :].bitcast(F32), 0.0).then_inc(warm_ready, 1)
            dve.memset(k_rows[ROWS_PROD:P, 0:NG // 2, :, :].bitcast(F32), TWO_ONES)

            def mask_rows():
                dve.wait_ge(mask_loaded, 16)
                dve.tensor_scalar(mask_bias[:, :], mask_in[:, :], -1.0, MASKED, ALU.add, ALU.mult).then_inc(setup_chain, 1)
                dve.wait_ge(setup_chain, 2)
                dve.tensor_copy(mask_parts[:, 0, :], mask_bias[:, :]).then_inc(setup_chain, 1)
                dve.wait_ge(setup_chain, 3)
                dve.tensor_tensor(mask_rest[:, 0, :], mask_bias[:, :], mask_parts[:, 0, :], ALU.subtract).then_inc(setup_chain, 1)
                dve.wait_ge(setup_chain, 4)
                dve.tensor_copy(mask_parts[:, 1, :], mask_rest[:, 0, :]).then_inc(setup_chain, 1)
                dve.wait_ge(setup_chain, 5)
                dve.tensor_tensor(mask_rest[:, 1, :], mask_rest[:, 0, :], mask_parts[:, 1, :], ALU.subtract).then_inc(setup_chain, 1)
                dve.wait_ge(setup_chain, 6)
                dve.tensor_copy(mask_parts[:, 2, :], mask_rest[:, 1, :]).then_inc(maskp_ready, 1)
                dve.memset(k_rows[ROWS_PROD:P, NG // 2:NG, :, :].bitcast(F32), TWO_ONES).then_inc(k_preset, 1)

            def silu_of_cond():
                dve.wait_ge(tanh_ready, 1)
                dve.scalar_tensor_tensor(cond_tanh[:, :], cond_tanh[:, :], 1.0, cond_in[:, :], ALU.add, ALU.mult
                                         ).then_inc(setup_chain, 1)
                dve.wait_ge(setup_chain, 1)
                dve.tensor_scalar(cond_silu[:, :], cond_tanh[:, :], 0.5, None, ALU.mult).then_inc(silu_ready, 1)
                dve.wait_ge(mask_turned, 1)
                dve.tensor_copy(mask_col[:, :, :], st_ps[0][:, 0:CH * B].rearrange("p (c b) -> p c b", b=B)
                                ).then_inc(mask_col_ready, 1)

            def embedding():
                dve.wait_ge(emb_ready, 2 * KD)
                for m in range(2 * KD):
                    dve.tensor_scalar(emb_t[:, m, :], job_ps[0][:, m * B:(m + 1) * B], eb_col[:, m:m + 1],
                                      1.0 if m < KD else 0.0, ALU.add, ALU.add).then_inc(setup_chain, 1)
                dve.wait_ge(setup_chain, 6 + 2 * KD)
                for k in range(KD):
                    dve.tensor_scalar(mod_full[:, 0, k, :], emb_t[:, k, :], sbw_col[:, k:k + 1], None, ALU.mult)
                    dve.scalar_tensor_tensor(mod_full[:, 1, k, :], emb_t[:, k, :], sbb_col[:, k:k + 1], emb_t[:, KD + k, :],
                                             ALU.mult, ALU.add).then_inc(setup_chain, 1)
                dve.wait_ge(setup_chain, 6 + 3 * KD)
                dve.tensor_scalar(mod_half[:, :, :, :], mod_full[:, :, :, :], 0.5, None, ALU.mult).then_inc(setup_done, 1)

            def max_unit(b, t, h):
                ahead = t + MAX_LEAD
                mb, step = (b, ahead) if ahead < STEPS else (b + 1, ahead - STEPS)
                if not exists(mb):
                    return
                g, c = step // CH, step % CH
                if c == 0 and h == 0:
                    wait(dve, turned["cturn"], NG * mb + g - 1)
                dve.wait_ge(max_ready, UNITS * mb + GH * step + h + 1)
                dve.tensor_reduce(negmax[:, g % 2, h * CH + c:h * CH + c + 1], mx_ps[bank_of(GH * step + h, MX_BANKS)][:, :],
                                  AXIS_X, ALU.max, negate=True).then_inc(max_done, 1)

            def stats(src, raw, c):
                dve.bn_stats(raw[:, c, :], src[:, c, :]).then_inc(bn_ready, 1)

            def moments(raw, mv, negmean, vareps, ready, nth):
                dve.wait_ge(bn_ready, 2 * CH * nth + CH)
                dve.memset(spacer[:, :], 0.0)
                for c in range(CH):
                    dve.bn_aggr(mv[:, c, :], raw[:, c, :]).then_inc(bn_ready, 1)
                dve.wait_ge(bn_ready, 2 * CH * (nth + 1))
                dve.tensor_scalar(negmean[:, :], mv[:, :, 0], -1.0, None, ALU.mult)
                dve.tensor_scalar(vareps[:, :], mv[:, :, 1], EPS, None, ALU.add).then_inc(ready, 1)

            def half_norm(src, dst, negmean, rstd, rstd_ready, norm_ready, d):
                dve.wait_ge(rstd_ready, d + 1)
                for c in range(CH // 2, CH):
                    dve.tensor_scalar(dst[:, c, :], src[:, c, :], negmean[:, c:c + 1], rstd[:, c:c + 1],
                                      ALU.add, ALU.mult).then_inc(norm_ready, 1)

            def split_max(at, b):
                _, _, kind, i, db = JOBS[at]
                if not job_exists(kind, i, db, b):
                    return
                ps, n = job_ps[at % JOB_BANKS], NG * b + i
                dve.wait_ge(turned["cturn"], n + 1)
                if not isinstance(b, int) or n >= 2:
                    lap, slot = (b, i - 2) if i >= 2 else (b - 1, i - 2 + NG)
                    dve.wait_ge(max_filled[slot], 2 * 16 * (lap + 1))
                dve.tensor_copy(max_parts[:, i % 2, 0, :], ps[0:GH * CH, 0:P]).then_inc(split_chain, 1)
                dve.wait_ge(split_chain, n + 1)
                dve.tensor_tensor(max_parts[:, i % 2, 1, :], ps[0:GH * CH, 0:P], max_parts[:, i % 2, 0, :],
                                  ALU.subtract).then_inc(max_split, 1)

            def read_job(at, b):
                _, _, kind, i, db = JOBS[at]
                if not job_exists(kind, i, db, b):
                    return
                ps, d = job_ps[at % JOB_BANKS], b + db
                if kind == "yturn":
                    by_head = ps[:, :].rearrange("p (c h w) -> p c h w", h=GH, w=VW)
                    dve.wait_ge(turned["yturn"], NG * d + i + 1)
                    wait(dve, y_ready, NG * d + i)
                    dve.reciprocal(y_recip[:, :, :], by_head[:, :, :, HD]).then_inc(recip_ready, 1)
                    dve.wait_ge(recip_ready, NG * d + i + 1)
                    wait(dve, y_norm_ready, CH * d)
                    dve.tensor_tensor(y[:, :, i * GC:(i + 1) * GC].rearrange("p c (h l) -> p c h l", l=HD),
                                      by_head[:, :, :, 0:HD],
                                      y_recip[:, :, :].unsqueeze(3).broadcast_to((P, CH, GH, HD)),
                                      ALU.mult).then_inc(y_ready, 1)
                elif kind == "outp":
                    dve.wait_ge(turned["outp"], 2 * d + i + 1)
                    dve.wait_ge(res_ready, d + 1)
                    wait(dve, out_saved, 2 * 16 * d)
                    dve.tensor_tensor(out_sb[:, 2 * i:2 * i + 2, :], ps[:, :].rearrange("p (c f) -> p c f", f=D),
                                      x_res[:, 2 * i:2 * i + 2, :], ALU.add).then_inc(out_ready, 1)

            def late_job(at, b):
                _, _, kind, i, db = JOBS[at]
                if not job_exists(kind, i, db, b):
                    return
                d = b + db
                if kind == "proj":
                    n = NG * d + i
                    dve.wait_ge(rest_ready, n + 1)
                    wait(dve, parts_saved[1], 16 * n)
                    dve.tensor_copy(qk_parts[:, 1, :], qk_rest[:, :]).then_inc(part1_ready, 1)
                elif kind == "hturn":
                    dve.wait_ge(h_lin_ready, KD * d + i + 1)
                    wait(dve, turned["outp"], 2 * d)
                    dve.scalar_tensor_tensor(h_t[:, i, :], h_tanh[:, i, :], 1.0, h_lin[:, i, :], ALU.add, ALU.mult
                                             ).then_inc(h_ready, 1)

            def x_stat(b, t, h):
                if not exists(b + 1) or (t, h) not in X_STAT:
                    return
                at = X_STAT.index((t, h))
                if at == 0:
                    dve.wait_ge(x_loaded, X_DMAS * 16 * (b + 2))
                    wait(dve, x_norm_ready, CH * (b + 1))
                if at < CH:
                    stats(x_in, x_stats, at)
                else:
                    moments(x_stats, x_mv, x_negmean, x_vareps, x_stat_ready, nth_stats(b, 0))
                    if isinstance(b, int) and b == -1:
                        half_norm(x_in, x_norm, x_negmean, x_rstd, x_rstd_ready, x_norm_ready, 0)

            def y_stat(b, t, h):
                if not exists(b - 1) or (t, h) not in Y_STAT:
                    return
                at = Y_STAT.index((t, h))
                if at == 0:
                    dve.wait_ge(y_ready, NG * b)
                    wait(dve, y_norm_ready, CH * (b - 1))
                if at < CH:
                    stats(y, y_stats, at)
                else:
                    moments(y_stats, y_mv, y_negmean, y_vareps, y_stat_ready, nth_stats(b, 1))
                    if isinstance(b, int) and b == B:
                        half_norm(y, y_norm, y_negmean, y_rstd, y_rstd_ready, y_norm_ready, B - 1)

            def body(b):
                for t in range(STEPS):
                    for h in range(GH):
                        max_unit(b, t, h)
                        if h == 0:
                            for n, at_b in jobs_at(b, t - 1, END):
                                read_job(n, at_b)
                        if h == 1:
                            for n, at_b in jobs_at(b, t, MID):
                                if JOBS[n][2] == "cturn":
                                    split_max(n, at_b)
                            for n, at_b in jobs_at(b, t - 2, END):
                                late_job(n, at_b)
                        x_stat(b, t, h)
                        y_stat(b, t, h)
                    if t == 1 and isinstance(b, int) and b == -1:
                        silu_of_cond()
                        mask_rows()
                    if t == TURN_STEP and isinstance(b, int) and b == -1:
                        dve.wait_ge(cond_turned, 1)
                        dve.tensor_copy(cond_t[:, :, :], st_ps[1][:, 0:KE * B].rearrange("p (k b) -> p k b", b=B)).then_inc(cond_ready, 1)
                    if t == 0 and isinstance(b, int) and b == 0:
                        embedding()

            def nth_stats(b, which):
                if not isinstance(b, int):
                    return 2 * b + which
                return sum(exists(i + 1) + exists(i - 1) for i in range(-1, b)) + (which if exists(b + 1) else 0)

            run(dve, body)

        @block.gpsimd
        def _(pool):
            pool.memset(ident[:, :], 1.0).then_inc(pool_chain, 1)
            pool.memset(exponent[:, :], -0.5)
            pool.wait_ge(pool_chain, 1)
            pool.affine_select(ident[:, :], ident[:, :], pattern=[[-1, P]], compare_op=ALU.is_equal, fill=0.0,
                               base=0, channel_multiplier=1).then_inc(consts_ready, 1)
            pool.wait_ge(consts_ready, 1)
            pool.memset(q_rows[ROWS_PROD:P, :, :, :].bitcast(F32), TWO_ONES).then_inc(q_preset, 1)
            pool.wait_ge(q_preset, 1)

            def presets():
                pool.memset(v_rows[:, :, :, :], 0.0).then_inc(pool_chain, 1)
                pool.wait_ge(pool_chain, 2)
                pool.memset(v_rows[:, :, :, HD:HD + 1], 1.0).then_inc(pool_chain, 1)
                pool.wait_ge(pool_chain, 3)

            def norm(src, dst, negmean, vareps, rstd, stat_ready, rstd_ready, norm_ready, d, chunks):
                pool.wait_ge(stat_ready, d + 1)
                pool.tensor_tensor(rstd[:, :], vareps[:, :], exponent[:, :], ALU.pow).then_inc(rstd_ready, 1)
                wait_apart(pool, consts_ready, rstd_ready, d + 1)
                for c in range(chunks):
                    pool.tensor_scalar(dst[:, c, :], src[:, c, :], negmean[:, c:c + 1], rstd[:, c:c + 1],
                                       ALU.add, ALU.mult).then_inc(norm_ready, 1)

            def take_rest(b, i, db):
                if not exists(b + db):
                    return
                n = NG * (b + db) + i
                pool.wait_ge(part0_ready, n + 1)
                wait(pool, part1_ready, n)
                wait(pool, part2_ready, n)
                pool.tensor_tensor(qk_rest[:, :], qk_full[:, :], qk_parts[:, 0, :], ALU.subtract).then_inc(rest_ready, 1)

            def take_part2(b, i, db):
                if not exists(b + db):
                    return
                n = NG * (b + db) + i
                pool.wait_ge(part1_ready, n + 1)
                wait(pool, parts_saved[2], 16 * n)
                pool.tensor_tensor(qk_parts[:, 2, :], qk_rest[:, :], qk_parts[:, 1, :], ALU.subtract).then_inc(part2_ready, 1)

            def values(b, g):
                if not exists(b):
                    return
                n = NG * b + g
                pool.wait_ge(v_plain_ready, 2 * (b + 1))
                wait(pool, v_ready, n)
                pool.tensor_tensor(v_biased[:, :, :], v_plain[:, :, g * GC:(g + 1) * GC],
                                   vb_row[:, g * GC:(g + 1) * GC].unsqueeze(1).broadcast_to((P, CH, GC)),
                                   ALU.add).then_inc(v_biased_ready, 1)
                pool.wait_ge(v_biased_ready, n + 1)
                wait(pool, pv_done, STEPS * (b - 1) + CH * (g + 1))
                pool.tensor_tensor(v_rows[:, :, g * GH:(g + 1) * GH, 0:HD],
                                   v_biased[:, :, :].rearrange("p c (h l) -> p c h l", l=HD),
                                   mask_now[:, :].unsqueeze(2).unsqueeze(3).broadcast_to((P, CH, GH, HD)),
                                   ALU.mult).then_inc(v_ready, 1)

            def body(b):
                if exists(b + 1):
                    wait(pool, turned["xturn"], KD * (b + 1))
                    norm(x_in, x_norm, x_negmean, x_vareps, x_rstd, x_stat_ready, x_rstd_ready, x_norm_ready, b + 1,
                         CH // 2 if isinstance(b, int) and b == -1 else CH)
                if isinstance(b, int) and b == -1:
                    presets()
                take_rest(b, 3, 0)
                take_part2(b, 3, 0)
                if exists(b - 1):
                    wait(pool, turned["hturn"], KD * (b - 1))
                    norm(y, y_norm, y_negmean, y_vareps, y_rstd, y_stat_ready, y_rstd_ready, y_norm_ready, b - 1,
                         CH // 2 if isinstance(b, int) and b == B else CH)
                    wait(pool, h_lin_ready, KD * (b - 1))
                    if isinstance(b, int) and b == 1:
                        pool.wait_ge(setup_done, 1)
                    pool.tensor_copy(mod_now[:, :, :], mod_half[:, :, :, bass.ds(b - 1, 1)].rearrange("p a k b -> p a (k b)")
                                     ).then_inc(mod_ready, 1)
                values(b, 3)
                if exists(b + 1):
                    if isinstance(b, int) and b == -1:
                        pool.wait_ge(mask_col_ready, 1)
                    wait_apart(pool, consts_ready, v_ready, NG * (b + 1))
                    pool.tensor_copy(mask_now[:, :], mask_col[:, :, bass.ds(b + 1, 1)].rearrange("p c b -> p (c b)")
                                     ).then_inc(now_ready, 1)
                take_rest(b, 0, 1)
                take_part2(b, 0, 1)
                if exists(b - 1):
                    pool.wait_ge(res_loaded, 16 * b)
                    pool.tensor_tensor(x_res[:, :, :], x_res[:, :, :],
                                       ob_row[:, :].unsqueeze(1).broadcast_to((P, CH, D)), ALU.add).then_inc(res_ready, 1)
                take_rest(b, 1, 1)
                take_part2(b, 1, 1)
                if exists(b + 1):
                    pool.wait_ge(now_ready, b + 2)
                values(b + 1, 0)
                take_rest(b, 2, 1)
                take_part2(b, 2, 1)
                values(b + 1, 1)
                values(b + 1, 2)

            run(pool, body)

        @block.sync
        def _(sp):
            for c in range(X_DMAS):
                sp.dma_start(x_in[:, 2 * c:2 * c + 2, :], batch_of(x_dram, 0)[:, 2 * c:2 * c + 2, :]).then_inc(x_loaded, 16)
            with nc.allow_non_contiguous_dma(reason="small vectors, once"):
                for dst, src in ((nb_col, norm_b), (nw_col, norm_w)):
                    sp.dma_start(dst[:, :], src.rearrange("(k p) -> p k", p=P)).then_inc(norm_loaded, 16)
                sp.dma_start(cond_in[:, :], cond[:, :]).then_inc(cond_loaded, 16)
                sp.dma_start(mask_in[:, :], mask[:, :]).then_inc(mask_loaded, 16)
                loads = [(w_qk[:, k, :, n * GC:(n + 1) * GC], w[k * P:(k + 1) * P, :].rearrange("p (g c) -> p g c", c=GC))
                         for k in range(KD) for n, w in enumerate((q_w, k_w))]
                for n, src in enumerate((q_b, k_b)):
                    loads.append((qkb_col[n * GC:(n + 1) * GC, :], src.rearrange("(g c) -> c g", c=GC)))
                loads.append((w_v[:, :, :], v_w.rearrange("(k p) n -> p k n", p=P)))
                loads.append((vb_row[:, :], v_b.rearrange("(a n) -> a n", a=1).broadcast_to((P, D))))
                assert len(loads) == WEIGHT_DMAS
                for dst, src in loads:
                    sp.dma_start(dst, src).then_inc(weights_loaded, 16)
                loads = [(sbw_col[:, :], sb_w.rearrange("(k p) -> p k", p=P)),
                         (sbb_col[:, :], sb_b.rearrange("(k p) -> p k", p=P)),
                         (eb_col[:, :], emb_b.rearrange("(k p) -> p k", p=P)),
                         (ob_row[:, :], out_b.rearrange("(a n) -> a n", a=1).broadcast_to((P, D))),
                         (w_e[:, :, :], emb_w.rearrange("(k p) n -> p k n", p=P)),
                         (w_o[:, :, :], out_w.rearrange("(k p) n -> p k n", p=P))]
                assert len(loads) == EMB_DMAS
                for dst, src in loads:
                    sp.dma_start(dst, src).then_inc(emb_loaded, 16)
            sp.wait_ge(maskp_ready, 1)
            sp.dma_start(mask_dram[:, :, :], mask_parts[:, :, :]).then_inc(mask_saved, 16)
            sp.wait_ge(mask_saved, 16)
            sp.wait_ge(q_preset, 1)
            sp.wait_ge(k_preset, 1)

            def spread(b, i, db):
                d = b + db
                if not exists(d):
                    return
                n = NG * d + i
                q_src, k_src = (qk_dram[i, :, :, m * GH:(m + 1) * GH, :].rearrange("s l h t -> s l (h t)") for m in range(2))

                def save(part, ready):
                    sp.wait_ge(ready, n + 1)
                    sp.dma_start(qk_dram[i, part].rearrange("l h t -> h l t"), qk_parts[:, part, :]
                                 ).then_inc(parts_saved[part], 16)

                def fill(part):
                    sp.wait_ge(parts_saved[part], 16 * (n + 1))
                    first, count = (0, 3, 5)[part], PARTS - part
                    sp.dma_start(k_rows[first * HD:(first + count) * HD, i, :, :].rearrange("p h t -> p (h t)"),
                                 k_src[part:part + 1].broadcast_to((count, HD, GH * T))).then_inc(rows_filled[i], 16)
                    first, count = (5, 3, 0)[part], part + 1
                    sp.dma_start(q_rows[first * HD:(first + count) * HD, i, :, :].rearrange("p h t -> p (h t)"),
                                 q_src[0:count]).then_inc(rows_filled[i], 16)

                save(0, part0_ready)
                sp.dma_start(k_rows[ROWS_PROD:ROWS_MASK, i, :, :],
                             mask_dram[bass.ds(d, 1)].rearrange("a s t -> (a s) t").unsqueeze(1).broadcast_to(
                                 (PARTS, GH, T))).then_inc(rows_filled[i], 16)
                save(1, part1_ready)
                save(2, part2_ready)
                fill(0)
                fill(1)
                fill(2)

            def body(b):
                if exists(b - 1):
                    wait_apart(sp, maskp_ready, out_ready, 2 * (b - 1))
                    sp.dma_start(x_res[:, :, :], batch_of(x_dram, b - 1)).then_inc(res_loaded, 16)
                spread(b, 3, 0)
                spread(b, 0, 1)
                if exists(b + 2):
                    wait_apart(sp, maskp_ready, x_norm_ready, CH * (b + 2))
                    for c in range(X_DMAS):
                        sp.dma_start(x_in[:, 2 * c:2 * c + 2, :], batch_of(x_dram, b + 2)[:, 2 * c:2 * c + 2, :]
                                     ).then_inc(x_loaded, 16)
                spread(b, 1, 1)
                for i in range(2):
                    if exists(b - 1):
                        wait_apart(sp, maskp_ready, out_ready, 2 * (b - 1) + i + 1)
                        sp.dma_start(batch_of(out_dram, b - 1)[:, 2 * i:2 * i + 2, :], out_sb[:, 2 * i:2 * i + 2, :]
                                     ).then_inc(out_saved, 16)
                    if i == 0:
                        spread(b, 2, 1)

            run(sp, body, B - 2)
            sp.wait_ge(out_saved, 2 * 16 * B)


_INS = ["x", "cond_2048", "mask_BxS_ff1", "L0_cond_norm_w", "L0_cond_norm_b", "L0_cond_q_w", "L0_cond_q_b",
        "L0_cond_k_w", "L0_cond_k_b", "L0_cond_v_w", "L0_cond_v_b", "L0_cond_emb_w", "L0_cond_emb_b",
        "L0_cond_sb_norm_w", "L0_cond_sb_norm_b", "L0_cond_out_w", "L0_cond_out_b"]


def kernel(**inputs):
    import numpy as _np
    import concourse.bacc as _bacc
    from concourse import mybir as _mybir
    from concourse.bass_utils import run_bass_kernel_spmd as _run

    nc = _bacc.Bacc("TRN2", target_bir_lowering=False, num_devices=1)
    arrays, args = {}, []
    for name in _INS:
        a = _np.ascontiguousarray(inputs[name])
        arrays[f"in_{name}"] = a
        args.append(nc.dram_tensor(f"in_{name}", a.shape, _mybir.dt.from_np(a.dtype), kind="ExternalInput").ap())
    args.append(nc.dram_tensor("out_0", (B, T, D), F32, kind="ExternalOutput").ap())
    attention_layer(nc, *args)
    r = _run(nc, [arrays], core_ids=[0])
    return r.results[0]["out_0"]
```
